# Optimizing a Trainium2 kernel written in Bass

```python
import numpy as np
import jax
import jax.numpy as jnp

def _softmax(x, axis=-1):
    return jax.nn.softmax(x, axis=axis)

def _gelu(x):
    return jax.nn.gelu(x, approximate=True)

def _silu(x):
    return jax.nn.silu(x)

def _sigmoid(x):
    return jax.nn.sigmoid(x)

def _layernorm(x, axis=-1, eps=1e-05):
    m = jnp.mean(x, axis=axis, keepdims=True)
    v = jnp.var(x, axis=axis, keepdims=True)
    return (x - m) / jnp.sqrt(v + eps)

def _scatter_add(tgt, idx, src, axis=0):
    return tgt.at[idx].add(src)

def _segment_sum(src, seg, n):
    return jax.ops.segment_sum(src, seg, n)
kernel_name = 'mk_adj_ffn_d1_adj_r2_adc160'

def setup_inputs(seed: int=0):
    np.random.seed(seed)
    _w = jnp.asarray

    def _rec_inputs():
        import jax
        import jax.numpy as jnp
        _gk = jax.random.key(seed)
        x = -0.0005207 + 1.001 * jax.random.normal(jax.random.fold_in(_gk, 1), (2048, 256), jnp.float32)
        _a = jax.random.bernoulli(jax.random.fold_in(_gk, 2), 0.00390625, (2048, 2048))
        adj = _a.astype(jnp.int32)
        return (x, adj)
    x, adj = _rec_inputs()

    def _L0_gnn_setup():
        import jax, jax.numpy as jnp
        import numpy as np
        HEAD_SIZE = 8
        QK_DIM = 256
        V_DIM = 256
        N = 2048
        ATT_DIM = QK_DIM // HEAD_SIZE
        SCALE = ATT_DIM ** (-0.5)
        NEG_FILL = jnp.float32(-9000000000000000.0)
        key = jax.random.key(seed)
        k1, k2, k3, k4 = jax.random.split(key, 4)
        x1 = jax.random.normal(k1, (N, QK_DIM), dtype=jnp.float32)
        x2 = jax.random.normal(k2, (N, QK_DIM), dtype=jnp.float32)
        v = jax.random.normal(k3, (N, V_DIM), dtype=jnp.float32)
        adj = jax.random.randint(k4, (N, N), 0, 2, dtype=jnp.int32)
        return {'x1': x1, 'x2': x2, 'v': v, 'adj': adj}
    _L0_gnn_all = _L0_gnn_setup()
    _L0_gnn_in = {k: v for k, v in _L0_gnn_all.items() if k in ('x2', 'v')}
    del _L0_gnn_all

    def _L0_ffn_setup():
        import jax, jax.numpy as jnp
        import numpy as np
        TOP_K = 2
        key = jax.random.key(seed)
        ks = jax.random.split(key, 7)
        B, S, D = (4, 2048, 256)
        E, H = (16, 4 * 256)
        s_in = 1.0 / np.sqrt(D)
        s_h = 1.0 / np.sqrt(H)
        return {'x': jax.random.normal(ks[0], (B, S, D), dtype=jnp.float32), 'Wg': jax.random.normal(ks[1], (D, E), dtype=jnp.float32) * s_in, 'bg': jnp.zeros((E,), dtype=jnp.float32), 'W1': jax.random.normal(ks[2], (E, D, H), dtype=jnp.float32) * s_in, 'b1': jnp.zeros((E, H), dtype=jnp.float32), 'W2': jax.random.normal(ks[3], (E, H, D), dtype=jnp.float32) * s_h, 'b2': jnp.zeros((E, D), dtype=jnp.float32)}
    _L0_ffn_all = _L0_ffn_setup()
    _L0_ffn_in = {k: v for k, v in _L0_ffn_all.items() if k in ('Wg', 'bg', 'W1', 'b1', 'W2', 'b2')}
    del _L0_ffn_all
    return {'x': x, 'adj': adj, 'L0_gnn_x2': _L0_gnn_in['x2'], 'L0_gnn_v': _L0_gnn_in['v'], 'L0_ffn_Wg': _L0_ffn_in['Wg'], 'L0_ffn_bg': _L0_ffn_in['bg'], 'L0_ffn_W1': _L0_ffn_in['W1'], 'L0_ffn_b1': _L0_ffn_in['b1'], 'L0_ffn_W2': _L0_ffn_in['W2'], 'L0_ffn_b2': _L0_ffn_in['b2']}

def reference(x, adj, L0_gnn_x2, L0_gnn_v, L0_ffn_Wg, L0_ffn_bg, L0_ffn_W1, L0_ffn_b1, L0_ffn_W2, L0_ffn_b2):
    import jax
    import jax.numpy as jnp

    def _L0_gnn_ref(x1, x2, v, adj):
        import jax, jax.numpy as jnp
        import numpy as np
        HEAD_SIZE = 8
        QK_DIM = 256
        V_DIM = 256
        N = 2048
        ATT_DIM = QK_DIM // HEAD_SIZE
        SCALE = ATT_DIM ** (-0.5)
        NEG_FILL = jnp.float32(-9000000000000000.0)
        n = x1.shape[0]
        q = x1.reshape(n, HEAD_SIZE, -1).transpose(1, 0, 2) * SCALE
        k = x2.reshape(n, HEAD_SIZE, -1).transpose(1, 0, 2)
        vv = v.reshape(n, HEAD_SIZE, -1).transpose(1, 0, 2)
        scores = jnp.einsum('hnd,hmd->hnm', q, k)
        scores = jnp.where(adj > 0, scores, NEG_FILL)
        attn = jax.nn.softmax(scores, axis=-1)
        out = jnp.einsum('hnm,hmd->hnd', attn, vv)
        return out.transpose(1, 0, 2).reshape(n, -1)

    def _L0_ffn_ref(x, Wg, bg, W1, b1, W2, b2):
        import jax, jax.numpy as jnp
        import numpy as np
        TOP_K = 2
        B, S, D = x.shape
        E = W1.shape[0]
        xf = x.reshape(-1, D)
        logits = xf @ Wg + bg
        w, idx = jax.lax.top_k(logits, TOP_K)
        w = jax.nn.softmax(w.astype(jnp.float32), axis=1).astype(x.dtype)
        onehot = jax.nn.one_hot(idx, E, dtype=x.dtype)
        combine = jnp.einsum('tk,tke->te', w, onehot)
        out = jnp.zeros_like(xf)
        for e in range(E):
            h = jax.nn.gelu(xf @ W1[e] + b1[e], approximate=False)
            y = h @ W2[e] + b2[e]
            out = out + combine[:, e:e + 1] * y
        return out.reshape(B, S, D)
    x = x + _L0_gnn_ref(_layernorm(x, axis=-1), L0_gnn_x2, L0_gnn_v, adj)
    x = x + _L0_ffn_ref(_layernorm(x, axis=-1)[None], L0_ffn_Wg, L0_ffn_bg, L0_ffn_W1, L0_ffn_b1, L0_ffn_W2, L0_ffn_b2)[0]
    return x

_drawn_inputs = setup_inputs


def setup_inputs(seed=0):
    import zlib

    import numpy as np

    out = dict(_drawn_inputs(seed))
    spreads = {'L0_ffn_bg': (0.0, 0.1), 'L0_ffn_b1': (0.0, 0.1), 'L0_ffn_b2': (0.0, 0.1)}
    factors = {}
    for name, (base, spread) in spreads.items():
        noise = np.random.default_rng([zlib.crc32(name.encode()), seed]).standard_normal(out[name].shape)
        drawn = base * np.exp(spread * noise) if base else spread * noise
        out[name] = jnp.asarray(drawn.astype(out[name].dtype))
    for name, factor in factors.items():
        out[name] = (out[name] * factor).astype(out[name].dtype)
    return out
```

```python
from contextlib import ExitStack
import concourse.bass as bass
from concourse import mybir
F32, F32R, BF16, I32, U32 = mybir.dt.float32, mybir.dt.float32r, mybir.dt.bfloat16, mybir.dt.int32, mybir.dt.uint32
ALU = mybir.AluOpType
ACT = mybir.ActivationFunctionType
AX = mybir.AxisListType


def graph_attention(nc, x, adj, x2, v, x1):
    N, D = x.shape
    H = 8
    DH = D // H
    P = 128
    NT = N // P
    KS = 3 * DH
    HALF = N // 2
    BANK = 512
    GRP = N // BANK
    BPG = BANK // P
    BATCH = 4
    SM = 4
    SCALE = DH ** -0.5
    MASKED = 9000000000000000.0
    EPS = 1e-5

    x_t = x.rearrange("(t p) d -> t p d", p=P)
    x_p = x.rearrange("(t p) d -> p t d", p=P)
    x2_p = x2.rearrange("(t p) d -> p t d", p=P)
    v_p = v.rearrange("(t p) d -> p t d", p=P)
    adj_t = adj.rearrange("(t p) m -> t p m", p=P)
    x1_t = x1.rearrange("(t p) d -> t p d", p=P)

    ctx = ExitStack()
    with ctx:
        def sb(name, shape, dt):
            return ctx.enter_context(nc.sbuf_tensor(name, shape, dt))

        def sem(name):
            return ctx.enter_context(nc.semaphore(name))

        keysT = sb("keysT", [KS, H, N], F32R)
        scores = sb("scores", [P, SM, N], F32)
        probsT = sb("probsT", [P, H, NT, P], F32)
        values = sb("values", [P, NT, D], F32)
        adj_bf = sb("adj_bf", [P, N], BF16)
        mask = sb("mask", [P, N], BF16)
        queriesT = sb("queriesT", [KS, H, P], F32R)
        q_nat = sb("q_nat", [P, H, 3, DH], F32R)
        x_q = sb("x_q", [P, D], F32)
        x_mid = sb("x_mid", [P, D], F32)
        xn = sb("xn", [P, D], F32)
        x_res = sb("x_res", [P, D], F32)
        att = sb("att", [P, D], F32)
        x1_sb = sb("x1_sb", [P, D], F32)
        outT = sb("outT", [P, 2, P], F32)
        ident = sb("ident", [P, P], F32)
        row_min = sb("row_min", [P, 2, 4], F32)
        row_sum = sb("row_sum", [P, NT * H], F32)
        r_den = sb("r_den", [P, H], F32)
        stats = sb("stats", [P, NT, 6], F32)
        mean_var = sb("mean_var", [P, NT, 2], F32)
        veps = sb("veps", [P, NT], F32)
        rv = sb("rv", [P, NT], F32)
        rstd = sb("rstd", [P, NT], F32)
        newton = sb("newton", [P, NT], F32)
        nscale = sb("nscale", [P, NT], F32)
        x_all = probsT[:, 0:2, :, :].rearrange("p a t n -> p (a t n)").rearrange("p (t d) -> p t d", d=D)
        x2_all = scores[:, 0:2, :].rearrange("p a n -> p (a n)").rearrange("p (t d) -> p t d", d=D)
        k_nat = [scores[:, 2 + i, 0:H * KS].rearrange("p (h c d) -> p h c d", c=3, d=DH).bitcast(F32R) for i in range(2)]

        s_ps = [ctx.enter_context(nc.psum_tensor(f"s_ps{i}", [P, HALF], F32)) for i in range(2)]
        t_ps = [ctx.enter_context(nc.psum_tensor(f"t_ps{i}", [P, BANK], F32)) for i in range(2)]
        o_ps = ctx.enter_context(nc.psum_tensor("o_ps", [P, BANK], F32))
        a_ps = ctx.enter_context(nc.psum_tensor("a_ps", [P, BANK], F32))

        x_in, v_in = sem("x_in"), sem("v_in")
        x2_in = [sem(f"x2_in{i}") for i in range(4)]
        ident_zero, ident_ready = sem("ident_zero"), sem("ident_ready")
        k_hi, k_split, k_tr, k_ev = sem("k_hi"), sem("k_split"), sem("k_tr"), sem("k_ev")
        ln_step, rv_ready, rs_ready, ln_ready = sem("ln_step"), sem("rv_ready"), sem("rs_ready"), sem("ln_ready")
        adj_in, xq_in, xr_in, x1_out = sem("adj_in"), sem("xq_in"), sem("xr_in"), sem("x1_out")
        mask_done, dve_waited = sem("mask_done"), sem("dve_waited")
        xn_done, hi_done, q_split = sem("xn_done"), sem("hi_done"), sem("q_split")
        q_tr, q_ev = sem("q_tr"), sem("q_ev")
        s_done, first_min, row_ready, exp_done = sem("s_done"), sem("first_min"), sem("row_ready"), sem("exp_done")
        t_done, dve_ev, act_ev = sem("t_done"), sem("dve_ev"), sem("act_ev")
        pv_done, outT_ev, o_tr = sem("pv_done"), sem("outT_ev"), sem("o_tr")
        den_ready, att_ready, x1_ready = sem("den_ready"), sem("att_ready"), sem("x1_ready")

        DVE_GROUPS = [(0,), (0, 2)]
        ACT_GROUPS = [(1, 2, 3), (1, 3)]

        def copied(groups, it, h, g=GRP - 1):
            per = sum(len(groups[i % 2]) for i in range(H))
            return it * per + sum(len(groups[i % 2]) for i in range(h)) + sum(1 for i in groups[h % 2] if i <= g)

        FIRST, MID, LAST, DRAIN = range(4)

        def back(phase, it, h, d):
            if phase == FIRST and h < d or phase == DRAIN and h >= d:
                return None
            return (it, h - d) if h >= d else (it - 1, h - d + H)

        def wait(eng, s, value):
            if not isinstance(value, int) or value > 0:
                eng.wait_ge(s, value)

        def tiles(eng, step):
            step(FIRST, 0)
            step(MID, 1)
            with eng.Fori(2, NT - 1) as it:
                step(MID, it)
            step(LAST, NT - 1)
            step(DRAIN, NT)

        def key_tiles(eng, step):
            step(0)
            with eng.Fori(1, NT // 2) as j:
                step(j)

        block = ctx.enter_context(nc.Block())

        @block.sync
        def _(sp):
            sp.dma_start(x_all, x_p).then_inc(x_in, 16)
            for i in range(4):
                sp.dma_start(x2_all[:, 4 * i:4 * i + 4, :], x2_p[:, 4 * i:4 * i + 4, :]).then_inc(x2_in[i], 16)
            sp.dma_start(x_q[:, :], x_t[0]).then_inc(xq_in, 16)
            sp.dma_start(values[:, :, :], v_p).then_inc(v_in, 16)

            def tile(phase, it):
                if phase in (FIRST, MID):
                    wait(sp, xn_done, it + 1)
                    sp.dma_start(x_q[:, :], x_t[it + 1]).then_inc(xq_in, 16)
                if phase != FIRST:
                    wait(sp, x1_ready, it - 1)
                    sp.dma_start(x_res[:, :], x_t[it - 1]).then_inc(xr_in, 16)
                    wait(sp, x1_ready, it)
                    sp.dma_start(x1_t[it - 1], x1_sb[:, :]).then_inc(x1_out, 16)

            tiles(sp, tile)
            sp.wait_ge(x1_out, 16 * NT)

        @block.gpsimd
        def _(pool):
            pool.dma_start(adj_bf[:, :], adj_t[0]).then_inc(adj_in, 16)
            nc.gpsimd.memset(ident[:, :], 0.0).then_inc(ident_zero, 1)
            pool.wait_ge(ident_zero, 1)
            nc.gpsimd.affine_select(out=ident[:, :], in_=ident[:, :], compare_op=ALU.not_equal, fill=1.0, base=0,
                                    pattern=[[-1, P]], channel_multiplier=1).then_inc(ident_ready, 1)

            for i in range(4):
                pool.wait_ge(x2_in[i], 16)

            def key_lows(j):
                for i in range(2):
                    t = 2 * j + i
                    wait(pool, k_hi, 2 * t + 2)
                    nc.gpsimd.tensor_tensor(out=k_nat[i][:, :, 1, :],
                                            in0=x2_all[:, bass.ds(t, 1), :].rearrange("p a (h d) -> p (a h) d", d=DH),
                                            in1=k_nat[i][:, :, 0, :].bitcast(F32), op=ALU.subtract).then_inc(k_split, 1)

            key_tiles(pool, key_lows)

            def split_queries(t):
                wait(pool, xq_in, 16 * t + 16)
                if isinstance(t, int) and t == 0:
                    pool.wait_ge(ln_ready, 1)
                wait(pool, q_split, t)
                row = [P, D]
                nc.gpsimd.tensor_tensor(out=x_mid[:, :], in0=x_q[:, :], in1=mean_var[:, bass.ds(t, 1), 0].to_broadcast(row),
                                        op=ALU.subtract).then_inc(xn_done, 1)
                wait(pool, xn_done, t + 1)
                wait(pool, q_tr, 2 * t)
                scale = nscale[:, bass.ds(t, 1)].to_broadcast(row)
                nc.gpsimd.tensor_tensor(out=xn[:, :], in0=x_mid[:, :], in1=scale, op=ALU.mult)
                for c in range(2):
                    nc.gpsimd.tensor_tensor(out=q_nat[:, :, c, :], in0=x_mid[:, :].rearrange("p (h d) -> p h d", d=DH),
                                            in1=nscale[:, bass.ds(t, 1)].unsqueeze(2).to_broadcast([P, H, DH]),
                                            op=ALU.mult).then_inc(hi_done, 1)
                wait(pool, hi_done, 2 * t + 2)
                nc.gpsimd.tensor_tensor(out=q_nat[:, :, 2, :], in0=xn[:, :].rearrange("p (h d) -> p h d", d=DH),
                                        in1=q_nat[:, :, 0, :].bitcast(F32), op=ALU.subtract).then_inc(q_split, 1)

            split_queries(0)

            def tile(phase, it):
                if phase in (FIRST, MID):
                    wait(pool, mask_done, it + 1)
                    pool.dma_start(adj_bf[:, :], adj_t[it + 1]).then_inc(adj_in, 16)
                    split_queries(it + 1)
                if phase != FIRST:
                    wait(pool, xr_in, 16 * it)
                    wait(pool, att_ready, it)
                    wait(pool, x1_out, 16 * (it - 1))
                    nc.gpsimd.tensor_tensor(out=x1_sb[:, :], in0=att[:, :], in1=x_res[:, :], op=ALU.add).then_inc(x1_ready, 1)

            tiles(pool, tile)

        @block.scalar
        def _(act):
            for i in range(4):
                act.wait_ge(x2_in[i], 16)

            def key_highs(j):
                for i in range(2):
                    t = 2 * j + i
                    if not isinstance(j, int):
                        act.wait_ge(k_tr, t - 1)
                    for c in (0, 2):
                        nc.scalar.copy(k_nat[i][:, :, c, :],
                                       x2_all[:, bass.ds(t, 1), :].rearrange("p a (h d) -> p (a h) d", d=DH)).then_inc(k_hi, 1)

            key_tiles(act, key_highs)
            act.wait_ge(rv_ready, 1)
            nc.scalar.activation(rstd[:, :], rv[:, :], ACT.Sqrt).then_inc(rs_ready, 1)

            def copy_queries(t, half):
                wait(act, q_tr, 2 * t + half + 1)
                wait(act, s_done, 2 * (H * (t - 1) + BATCH * half + BATCH))
                nc.scalar.copy(queriesT[:, BATCH * half:BATCH * half + BATCH, :],
                               a_ps[0:KS, :].rearrange("p (h n) -> p h n", n=P)).then_inc(q_ev, 1)

            copy_queries(0, 0)

            def tile(phase, it):
                for h in range(H):
                    if phase in (FIRST, MID, LAST) and h == 0:
                        copy_queries(it, 1)
                    prev = back(phase, it, h, 1)
                    if prev is not None:
                        t, g = prev
                        wait(act, row_ready, H * t + g + 1)
                        buf = scores[:, g % SM, :]
                        nc.scalar.activation(buf, buf, ACT.Exp, bias=row_min[:, 1, g % 4:g % 4 + 1], scale=-1.0,
                                             accum_out=row_sum[:, bass.ds(t * H + g, 1)]).then_inc(exp_done, 1)
                    prev = back(phase, it, h, 2)
                    if prev is not None:
                        t, g = prev
                        for grp in ACT_GROUPS[g % 2]:
                            wait(act, t_done, GRP * (H * t + g) + grp + 1)
                            slot_free(act, phase, t, g)
                            nc.scalar.copy(probsT[:, g, BPG * grp:BPG * grp + BPG, :],
                                           t_ps[grp % 2][:, :].rearrange("p (c n) -> p c n", n=P)).then_inc(act_ev, 1)
                    if phase in (FIRST, MID) and h == 4:
                        copy_queries(it + 1, 0)

            def slot_free(eng, phase, t, g):
                if not (isinstance(t, int) and t == 0):
                    eng.wait_ge(pv_done, 2 * t - 1 + g // BATCH)

            tiles(act, tile)

        @block.vector
        def _(dve):
            n_ln = [0]

            def ln(ins):
                n_ln[0] += 1
                ins.then_inc(ln_step, 1)
                dve.wait_ge(ln_step, n_ln[0])

            dve.wait_ge(x_in, 16)
            for t in range(NT):
                last = nc.vector.bn_stats(out=stats[:, t, :], in_=x_all[:, t, :])
            ln(last)
            for t in range(NT):
                last = nc.vector.bn_aggr(out=mean_var[:, t, :], in_=stats[:, t, :])
            ln(last)
            ln(nc.vector.tensor_scalar(veps[:, :], mean_var[:, :, 1], EPS, None, ALU.add))
            ln(nc.vector.reciprocal(rv[:, :], veps[:, :]))
            nc.vector.tensor_scalar(rv[:, :], rv[:, :], 1.0, None, ALU.mult).then_inc(rv_ready, 1)

            def copy_keys(j):
                for i in range(2):
                    t = 2 * j + i
                    dve.wait_ge(k_tr, t + 1)
                    nc.vector.tensor_copy(out=keysT[:, :, bass.ds(t * P, P)],
                                          in_=s_ps[i][0:KS, :].rearrange("p (h n) -> p h n", n=P)).then_inc(k_ev, 1)

            key_tiles(dve, copy_keys)
            dve.wait_ge(rs_ready, 1)
            ln(nc.vector.tensor_tensor(newton[:, :], rstd[:, :], rstd[:, :], ALU.mult))
            ln(nc.vector.tensor_tensor(newton[:, :], newton[:, :], veps[:, :], ALU.mult))
            ln(nc.vector.tensor_scalar(newton[:, :], newton[:, :], -0.5, 1.5, ALU.mult, ALU.add))
            ln(nc.vector.tensor_tensor(rstd[:, :], rstd[:, :], newton[:, :], ALU.mult))
            nc.vector.tensor_scalar(nscale[:, :], rstd[:, :], -SCALE, None, ALU.mult).then_inc(ln_ready, 1)

            def slot_free(eng, t, g):
                if not (isinstance(t, int) and t == 0):
                    eng.wait_ge(pv_done, 2 * t - 1 + g // BATCH)

            def tile(phase, it):
                for h in range(H):
                    u = H * it + h
                    if phase != DRAIN:
                        if h == 0:
                            dve.wait_ge(adj_in, 16 * it + 16)
                            wait(dve, row_ready, u)
                            nc.vector.tensor_scalar(mask[:, :], adj_bf[:, :], 0.0, MASKED, ALU.is_le,
                                                    ALU.mult).then_inc(mask_done, 1)
                            dve.wait_ge(mask_done, it + 1)
                        dve.wait_ge(s_done, 2 * u + 1)
                        if back(phase, it, h, SM) is not None:
                            dve.wait_ge(t_done, GRP * (u - SM) + GRP)
                        dve.sem_inc(dve_waited, 1)
                        nc.vector.tensor_tensor_reduce(
                            out=scores[:, h % SM, 0:HALF], in0=s_ps[0][:, :], in1=mask[:, 0:HALF], scale=1.0, scalar=3e38,
                            op0=ALU.add, op1=ALU.min, accum_out=row_min[:, 0, h % 4:h % 4 + 1]).then_inc(first_min, 1)
                    prev = back(phase, it, h, 2)
                    if prev is not None:
                        t, g = prev
                        slot_free(dve, t, g)
                        for grp in DVE_GROUPS[g % 2]:
                            if grp:
                                continue
                            dve.wait_ge(t_done, GRP * (H * t + g) + grp + 1)
                            nc.vector.tensor_copy(out=probsT[:, g, BPG * grp:BPG * grp + BPG, :],
                                                  in_=t_ps[grp % 2][:, :].rearrange("p (c n) -> p c n", n=P)).then_inc(dve_ev, 1)
                    if phase != DRAIN:
                        dve.wait_ge(s_done, 2 * u + 2)
                        dve.wait_ge(first_min, u + 1)
                        dve.sem_inc(dve_waited, 1)
                        dve.sem_inc(dve_waited, 1)
                        nc.vector.tensor_tensor_reduce(
                            out=scores[:, h % SM, HALF:N], in0=s_ps[1][:, :], in1=mask[:, HALF:N], scale=1.0,
                            scalar=row_min[:, 0, h % 4:h % 4 + 1], op0=ALU.add, op1=ALU.min,
                            accum_out=row_min[:, 1, h % 4:h % 4 + 1]).then_inc(row_ready, 1)
                    if prev is not None:
                        for grp in DVE_GROUPS[g % 2]:
                            if not grp:
                                continue
                            dve.wait_ge(t_done, GRP * (H * t + g) + grp + 1)
                            nc.vector.tensor_copy(out=probsT[:, g, BPG * grp:BPG * grp + BPG, :],
                                                  in_=t_ps[grp % 2][:, :].rearrange("p (c n) -> p c n", n=P)).then_inc(dve_ev, 1)
                    if phase != FIRST and h in (2, 6):
                        b = 2 * it - 2 + h // BATCH
                        dve.wait_ge(pv_done, b + 1)
                        wait(dve, o_tr, it - 1)
                        nc.vector.tensor_copy(out=outT[:, h // BATCH, :], in_=o_ps[:, 0:P]).then_inc(outT_ev, 1)
                    if phase != FIRST and h == 7:
                        dve.wait_ge(exp_done, H * it)
                        wait(dve, att_ready, it - 1)
                        nc.vector.reciprocal(r_den[:, :], row_sum[:, bass.ds((it - 1) * H, H)]).then_inc(den_ready, 1)
                        dve.wait_ge(den_ready, it)
                        dve.wait_ge(o_tr, it)
                        wait(dve, x1_ready, it - 1)
                        nc.vector.tensor_tensor(att[:, :].rearrange("p (h d) -> p h d", d=DH),
                                                a_ps[:, 0:D].rearrange("p (h d) -> p h d", d=DH),
                                                r_den[:, :].unsqueeze(2).to_broadcast([P, H, DH]), ALU.mult).then_inc(att_ready, 1)

            tiles(dve, tile)

        @block.tensor
        def _(pe):
            pe.wait_ge(ident_ready, 1)

            def transpose_keys(j):
                for i in range(2):
                    t = 2 * j + i
                    pe.wait_ge(k_split, t + 1)
                    pe.wait_ge(k_hi, 2 * t + 2)
                    if not isinstance(j, int):
                        pe.wait_ge(k_ev, t - 1)
                    for h in range(H):
                        last = nc.tensor.transpose(s_ps[i][0:KS, h * P:h * P + P],
                                                   k_nat[i][:, h, :, :].bitcast(F32).rearrange("p c d -> p (c d)"), ident[:, :])
                    last.then_inc(k_tr, 1)

            key_tiles(pe, transpose_keys)

            def transpose_queries(t, half):
                pe.wait_ge(q_split, t + 1)
                pe.wait_ge(hi_done, 2 * t + 2)
                if half == 0:
                    wait(pe, q_ev, 2 * t)
                else:
                    wait(pe, att_ready, t - 1)
                    pe.wait_ge(q_ev, 2 * t + 1)
                for i in range(BATCH):
                    last = nc.tensor.transpose(a_ps[0:KS, i * P:i * P + P],
                                               q_nat[:, BATCH * half + i, :, :].bitcast(F32).rearrange("p c d -> p (c d)"),
                                               ident[:, :])
                last.then_inc(q_tr, 1)

            def score(t, h, half):
                u = H * t + h
                if half == 0:
                    pe.wait_ge(q_ev, 2 * t + 1 + h // BATCH)
                    wait(pe, first_min, u)
                    if isinstance(t, int) and t == 0:
                        pe.wait_ge(k_ev, NT)
                else:
                    wait(pe, row_ready, u)
                for c in range(HALF // BANK):
                    m = half * HALF + c * BANK
                    last = nc.tensor.matmul(s_ps[half][:, c * BANK:c * BANK + BANK], queriesT[:, h, :], keysT[:, h, m:m + BANK],
                                            start=True, stop=True)
                last.then_inc(s_done, 1)

            def transpose_probs(t, h, grp):
                u = H * t + h
                if grp == 0:
                    pe.wait_ge(exp_done, u + 1)
                before = (t, h, grp - 2) if grp >= 2 else (t, h - 1, grp + 2) if h else (t - 1, H - 1, grp + 2)
                tt, hh, gg = before
                if gg in DVE_GROUPS[hh % 2]:
                    wait(pe, dve_ev, copied(DVE_GROUPS, tt, hh, gg))
                else:
                    wait(pe, act_ev, copied(ACT_GROUPS, tt, hh, gg))
                for i in range(BPG):
                    m = (grp * BPG + i) * P
                    last = nc.tensor.transpose(t_ps[grp % 2][:, i * P:i * P + P], scores[:, h % SM, m:m + P], ident[:, :])
                last.then_inc(t_done, 1)

            def value_products(t, half, quarter):
                if quarter == 0:
                    hh = BATCH * half + BATCH - 1
                    pe.wait_ge(dve_ev, copied(DVE_GROUPS, t, hh))
                    pe.wait_ge(act_ev, copied(ACT_GROUPS, t, hh))
                    wait(pe, outT_ev, 2 * t + half)
                    if isinstance(t, int) and t == 0:
                        pe.wait_ge(v_in, 16)
                for c in range(BPG * quarter, BPG * quarter + BPG):
                    for i in range(BATCH):
                        h = BATCH * half + i
                        last = nc.tensor.matmul(o_ps[DH * i:DH * i + DH, 0:P], values[:, c, h * DH:h * DH + DH],
                                                probsT[:, h, c, :], start=c == 0, stop=c == NT - 1,
                                                tile_position=(0, DH * i))
                if quarter == GRP - 1:
                    last.then_inc(pv_done, 1)

            def transpose_out(phase, t):
                pe.wait_ge(outT_ev, 2 * t + 2)
                pe.wait_ge(q_ev, 2 * NT if phase in (LAST, DRAIN) else 2 * t + 5)
                for half in range(2):
                    last = nc.tensor.transpose(a_ps[:, half * P:half * P + P], outT[:, half, :], ident[:, :])
                last.then_inc(o_tr, 1)

            transpose_queries(0, 0)
            score(0, 0, 0)
            score(0, 0, 1)

            def tile(phase, it):
                for h in range(H):
                    if phase != DRAIN and h == 0:
                        transpose_queries(it, 1)
                    ahead = phase in (FIRST, MID) or phase == LAST and h < H - 1
                    nxt = (it, h + 1) if h < H - 1 else (it + 1, 0)
                    prev = back(phase, it, h, 2)
                    if ahead:
                        score(*nxt, 0)
                    if prev is not None:
                        transpose_probs(*prev, 0)
                        transpose_probs(*prev, 1)
                    if ahead:
                        score(*nxt, 1)
                    if prev is not None:
                        transpose_probs(*prev, 2)
                        transpose_probs(*prev, 3)
                    if phase in (FIRST, MID) and h == 4:
                        transpose_queries(it + 1, 0)
                    if phase != FIRST and h == 7:
                        transpose_out(phase, it - 1)
                    if phase != FIRST or h >= 6:
                        q = (h - 6) % 4
                        if phase == DRAIN and h >= 6:
                            continue
                        t, half = (it, 0) if h >= 6 else (it - 1, 0 if h < 2 else 1)
                        value_products(t, half, q)

            tiles(pe, tile)


def expert_ffn(nc, x1, wg, bg, w1, b1, w2, b2, out, slots_x, slots_y):
    N, D = x1.shape
    E, _, HID = w1.shape
    P = 128
    NT = N // P
    TOPK = 2
    DC = D // P
    HC = HID // P
    BANK = 512
    TILES = slots_x.shape[0] // P
    assert TILES >= N * TOPK // P + E - 1 and TILES % 2 == 0 and N // P <= E
    EPS = 1e-5
    LOW = -3e38
    W1C, W2C = DC * HID, HC * D
    WC = W1C + W2C

    x1_p = x1.rearrange("(t p) d -> p t d", p=P)
    out_t = out.rearrange("(t p) d -> t p d", p=P)
    wg_p = wg.rearrange("(k p) e -> p k e", p=P)
    w1_p = w1.rearrange("e (k p) h -> e p k h", p=P)
    w2_p = w2.rearrange("e (p c) d -> e p (c d)", c=HC)
    sx_t = slots_x.rearrange("(i p) d -> i p d", p=P)
    sy_t = slots_y.rearrange("(i p) d -> i p d", p=P)

    ctx = ExitStack()
    with ctx:
        def sb(name, shape, dt):
            return ctx.enter_context(nc.sbuf_tensor(name, shape, dt))

        def sem(name):
            return ctx.enter_context(nc.semaphore(name))

        w_raw = sb("w_raw", [P, 2, WC], F32)
        w_hi = sb("w_hi", [P, 2 * WC], F32R)
        w_lo = sb("w_lo", [P, 2 * WC], F32R)
        b1_bc = sb("b1_bc", [P, 2 * HID], F32)
        b2_bc = sb("b2_bc", [P, 2 * D], F32)
        x1_all = sb("x1_all", [P, NT, D], F32)
        y_all = sb("y_all", [P, NT, D], F32)
        ident2 = sb("ident2", [P, P], F32)
        route = sb("route", [P, 16, NT, E], F32)
        small = sb("small", [P, 12, NT], F32)
        picks = sb("picks", [P, NT, E], BF16)
        before = sb("before", [P, P], BF16)
        ones = sb("ones", [P, P], BF16)
        wg_sb = sb("wg_sb", [P, DC, E], F32)
        bg_bc = sb("bg_bc", [P, E], F32)
        cum = sb("cum", [P, NT + 1, E], F32)
        slot_fp = sb("slot_fp", [P, TOPK, NT], F32)
        slot_of = sb("slot_of", [P, TOPK, NT], U32)
        tile_iota = sb("tile_iota", [1, TILES, E], F32)
        ended = sb("ended", [1, TILES, E], F32)
        tile_expert = sb("tile_expert", [1, TILES], F32)
        tile_expert_i = sb("tile_expert_i", [1, TILES], I32)
        tile_end_i = sb("tile_end_i", [1, E], I32)
        stats2 = sb("stats2", [P, NT, 6], F32)
        mv2 = sb("mv2", [P, NT, 2], F32)
        x_in_sb = sb("x_in_sb", [P, 2, D], F32)
        xT_hi = sb("xT_hi", [P, 2, DC * P], F32R)
        xT_lo = sb("xT_lo", [P, 2, DC * P], F32R)
        hid = sb("hid", [P, 2, HID], F32)
        hT_hi = sb("hT_hi", [P, 2, HID], F32R)
        hT_lo = sb("hT_lo", [P, 2, HID], F32R)
        y_sb = sb("y_sb", [P, 2, D], F32)
        yT = [hid[:, :, :].rearrange("p a h -> p (a h)"), sb("yT_second", [P, N], F32)[:, :]]
        GB = 4
        got = [[w_raw[:, k, i * D:i * D + D] for i in range(GB)] for k in range(TOPK)]
        res = [hid[:, 0, i * D:i * D + D] for i in range(2)]
        part = [hid[:, 1, i * D:i * D + D] for i in range(2)]

        logits, equal, cand, pick1, rest, pick2, pos, tmp, iota_e, iota_j, tri, zero = (route[:, i] for i in range(12))
        tiles_e, end_e, base_e = (route[:, 12, i, :] for i in range(3))
        max1, min1, max2, diff, ediff, wt1, wt2, veps2, rv2, rstd2, newton2, mean_n = (small[:, i, :] for i in range(12))

        h_ps = ctx.enter_context(nc.psum_tensor("h_ps", [P, HID], F32))
        ht_ps = ctx.enter_context(nc.psum_tensor("ht_ps", [P, HID], F32))
        y_ps = [ctx.enter_context(nc.psum_tensor(f"y_ps{i}", [P, BANK], F32)) for i in range(2)]
        xt_ps = ctx.enter_context(nc.psum_tensor("xt_ps", [P, BANK], F32))
        lg_ps = ctx.enter_context(nc.psum_tensor("lg_ps", [P, BANK], F32))

        x1_in, wg_in = sem("x1_in"), sem("wg_in")
        const_step, const_ready = sem("const_step"), sem("const_ready")
        step, rv_ready, rs_ready = sem("step"), sem("rv2_ready"), sem("rs2_ready")
        y_ready, yT_done, yT_dve, yT_act, lg_done = sem("y_ready"), sem("yT_done"), sem("yT_dve"), sem("yT_act"), sem("lg_done")
        picked, ranked, diff_ready, ediff_ready = sem("picked"), sem("ranked"), sem("diff_ready"), sem("ediff_ready")
        slots_ready, table_ready, scattered, zeroed, zero_ready = (sem("slots_ready"), sem("table_ready"), sem("scattered"),
                                                                   sem("zeroed"), sem("zero_ready"))
        raw_in = [sem(f"raw_in{i}") for i in range(2)]
        b_in = [sem(f"b_in{i}") for i in range(2)]
        pool_waited = sem("pool_waited")
        hi_ready, w_ready, bias_ready = sem("hi_ready"), sem("w_ready"), sem("bias_ready")
        sx_in = [sem(f"sx_in{i}") for i in range(2)]
        xt_done, x_hi, x_lo = sem("xt_done"), sem("x_hi"), sem("x_lo")
        h_done, h_biased, gelu_done = sem("h_done"), sem("h_biased"), sem("gelu_done")
        ht_done, h_hi, h_lo = sem("ht_done"), sem("h_hi"), sem("h_lo")
        y_done, y_biased = sem("y_done"), sem("y_biased")
        sy_out = [sem(f"sy_out{i}") for i in range(2)]
        gathered = [sem(f"gathered{i}") for i in range(GB)]
        part_ready, res_ready = sem("part_ready"), sem("res_ready")
        stored = [sem(f"stored{i}") for i in range(2)]

        def wait(eng, s, value):
            if not isinstance(value, int) or value > 0:
                eng.wait_ge(s, value)

        def steps(eng, pair):
            pair(0, 0)
            pair(1, 1)
            with eng.Fori(2, TILES // 2 - 1) as j:
                pair(1, j)
            pair(2, TILES // 2 - 1)
            pair(3, TILES // 2)

        def has(phase, i, d):
            if phase == 0:
                return i >= d
            if phase == 2:
                return i - d < 2
            if phase == 3:
                return i - d < 0
            return True

        def expert_of(eng, tile):
            return eng.value_load(tile_expert_i[0:1, bass.ds(tile, 1)], min_val=0, max_val=E - 1)

        block = ctx.enter_context(nc.Block())

        @block.sync
        def _(sp):
            sp.dma_start(x1_all[:, :, :], x1_p).then_inc(x1_in, 16)
            sp.dma_start(wg_sb[:, :, :], wg_p).then_inc(wg_in, 16)
            sp.dma_start(bg_bc[:, :], bg.rearrange("(a e) -> a e", a=1).to_broadcast([P, E])).then_inc(wg_in, 16)
            sp.wait_ge(zero_ready, 1)
            for i in range(TILES // NT):
                sp.dma_start(slots_x[i * N:i * N + N, :].rearrange("(p t) d -> p (t d)", p=P),
                             y_all[:, :, :].rearrange("p t d -> p (t d)")).then_inc(zeroed, 16)
            sp.wait_ge(scattered, 16 * TOPK * NT)
            for i in range(2):
                sp.dma_start(x_in_sb[:, i, :], sx_t[i]).then_inc(sx_in[i], 16)

            def pair(phase, j):
                for i in range(2):
                    s = 2 * j + i
                    if has(phase, i, -2) and phase != 2:
                        sp.wait_ge(xt_done, s + 1)
                        sp.dma_start(x_in_sb[:, i, :], sx_t[s + 2]).then_inc(sx_in[i], 16)
                    if has(phase, i, 2):
                        sp.wait_ge(y_biased, s)
                        sp.dma_start(sy_t[s - 2], y_sb[:, i, :]).then_inc(sy_out[i], 16)

            steps(sp, pair)
            for t in range(NT):
                sp.wait_ge(res_ready, t + 1)
                sp.dma_start(out_t[t], res[t % 2]).then_inc(stored[t % 2], 16)
            for i in range(2):
                sp.wait_ge(stored[i], 16 * NT // 2)

        @block.gpsimd
        def _(pool):
            def load_expert(e, i):
                pool.dma_start(w_raw[:, i, 0:W1C].rearrange("p (k h) -> p k h", k=DC),
                               w1_p[bass.ds(e, 1)].rearrange("a p k h -> p (a k) h")).then_inc(raw_in[i], 16)
                pool.dma_start(w_raw[:, i, W1C:WC], w2_p[bass.ds(e, 1)].rearrange("a p n -> p (a n)")).then_inc(raw_in[i], 16)

            def load_bias(e, i):
                pool.dma_start(b1_bc[:, i * HID:i * HID + HID], b1[bass.ds(e, 1), :].to_broadcast([P, HID])).then_inc(b_in[i], 16)
                pool.dma_start(b2_bc[:, i * D:i * D + D], b2[bass.ds(e, 1), :].to_broadcast([P, D])).then_inc(b_in[i], 16)

            n_c = [0]

            def const(ins):
                n_c[0] += 1
                ins.then_inc(const_step, 1)
                pool.wait_ge(const_step, n_c[0])

            for i in range(2):
                load_expert(i, i)
            for i in range(2):
                load_bias(i, i)
            const(nc.gpsimd.memset(ident2[:, :], 0.0))
            nc.gpsimd.affine_select(out=ident2[:, :], in_=ident2[:, :], compare_op=ALU.not_equal, fill=1.0, base=0,
                                    pattern=[[-1, P]], channel_multiplier=1)
            nc.gpsimd.memset(ones[:, :], 1.0)
            const(nc.gpsimd.memset(before[:, :], 1.0))
            nc.gpsimd.affine_select(out=before[:, :], in_=before[:, :], compare_op=ALU.is_gt, fill=0.0, base=0,
                                    pattern=[[1, P]], channel_multiplier=-1)
            nc.gpsimd.iota(iota_e, pattern=[[0, NT], [1, E]], base=0, channel_multiplier=0, allow_small_or_imprecise_dtypes=True)
            nc.gpsimd.iota(iota_j, pattern=[[0, E], [P, NT]], base=0, channel_multiplier=0, allow_small_or_imprecise_dtypes=True)
            nc.gpsimd.iota(tile_iota[:, :, :], pattern=[[1, TILES], [0, E]], base=0, channel_multiplier=0,
                           allow_small_or_imprecise_dtypes=True)
            const(nc.gpsimd.memset(tri, 1.0))
            nc.gpsimd.affine_select(out=tri, in_=tri, compare_op=ALU.is_ge, fill=0.0, base=0,
                                    pattern=[[1, E], [-1, E]], channel_multiplier=0).then_inc(const_ready, 1)

            pool.wait_ge(slots_ready, 1)
            pool.wait_ge(zeroed, 16 * (TILES // NT))
            pool.wait_ge(y_ready, NT)
            for k in range(TOPK):
                for t in range(NT):
                    pool.indirect_dma_start(out=slots_x[:, :], out_offset=bass.IndirectOffsetOnAxis(ap=slot_of[:, k, t:t + 1], axis=0),
                                            in_=y_all[:, t, :], in_offset=None).then_inc(scattered, 16)
            pool.wait_ge(table_ready, 1)

            def split(j, first, last):
                for i in range(2):
                    e = 2 * j + i
                    pool.wait_ge(raw_in[i], 32 * j + 32)
                    if not first:
                        done = pool.value_load(tile_end_i[0:1, bass.ds(e - 2, 1)], min_val=0, max_val=TILES)
                        pool.wait_ge(y_biased, done + 1)
                        pool.sem_inc(pool_waited, 1)
                        load_bias(e, i)
                    nc.gpsimd.tensor_copy(out=w_hi[:, i * WC:i * WC + WC], in_=w_raw[:, i, :]).then_inc(hi_ready, 1)
                    wait(pool, hi_ready, e + 1)
                    nc.gpsimd.tensor_tensor(out=w_lo[:, i * WC:i * WC + WC], in0=w_raw[:, i, :],
                                            in1=w_hi[:, i * WC:i * WC + WC].bitcast(F32), op=ALU.subtract).then_inc(w_ready, 1)
                    if not last:
                        pool.wait_ge(w_ready, e + 1)
                        load_expert(e + 2, i)
                    pool.wait_ge(b_in[i], 32 * j + 32)
                    pool.sem_inc(bias_ready, 1)

            split(0, True, False)
            with pool.Fori(1, E // 2 - 1) as j:
                split(j, False, False)
            split(E // 2 - 1, False, True)

            for i in range(2):
                pool.wait_ge(sy_out[i], 16 * TILES // 2)
            for t in range(NT):
                if t >= GB:
                    pool.wait_ge(res_ready, t - GB + 1)
                for k in range(TOPK):
                    pool.indirect_dma_start(out=got[k][t % GB], out_offset=None, in_=slots_y[:, :],
                                            in_offset=bass.IndirectOffsetOnAxis(ap=slot_of[:, k, t:t + 1], axis=0)
                                            ).then_inc(gathered[t % GB], 16)

        @block.scalar
        def _(act):
            act.wait_ge(rv_ready, 1)
            nc.scalar.activation(rstd2, rv2, ACT.Sqrt).then_inc(rs_ready, 1)
            for g in range(1, 8, 2):
                act.wait_ge(yT_done, g + 1)
                nc.scalar.copy(yT[g // 4][:, (g % 4) * BANK:(g % 4) * BANK + BANK], ht_ps[:, BANK:2 * BANK]).then_inc(yT_act, 1)
            act.wait_ge(diff_ready, 1)
            nc.scalar.activation(ediff, diff, ACT.Exp).then_inc(ediff_ready, 1)

            def pair(phase, j):
                for i in range(2):
                    s = 2 * j + i
                    if has(phase, i, 0):
                        act.wait_ge(h_biased, s + 1)
                        nc.scalar.activation(hid[:, i, :], hid[:, i, :], ACT.Gelu).then_inc(gelu_done, 1)
                    if has(phase, i, -1):
                        x_high(s + 1, 1 - i)
                    if has(phase, i, 1):
                        act.wait_ge(ht_done, s)
                        wait(act, y_done, s - 2)
                        nc.scalar.copy(hT_hi[:, 1 - i, :], ht_ps[:, :]).then_inc(h_hi, 1)

            def x_high(t, i):
                act.wait_ge(xt_done, t + 1)
                wait(act, h_done, t - 1)
                nc.scalar.copy(xT_hi[:, i, :], xt_ps[:, 0:DC * P]).then_inc(x_hi, 1)

            x_high(0, 0)
            steps(act, pair)

        @block.vector
        def _(dve):
            n = [0]

            def do(ins):
                n[0] += 1
                ins.then_inc(step, 1)
                dve.wait_ge(step, n[0])

            tt, ts, red = nc.vector.tensor_tensor, nc.vector.tensor_scalar, nc.vector.tensor_reduce
            nc.vector.memset(y_all[:, :, :], 0.0).then_inc(zero_ready, 1)
            dve.wait_ge(x1_in, 16)
            for t in range(NT):
                last = nc.vector.bn_stats(out=stats2[:, t, :], in_=x1_all[:, t, :])
            do(last)
            for t in range(NT):
                last = nc.vector.bn_aggr(out=mv2[:, t, :], in_=stats2[:, t, :])
            do(last)
            do(ts(veps2, mv2[:, :, 1], EPS, None, ALU.add))
            nc.vector.reciprocal(rv2, veps2).then_inc(rv_ready, 1)
            dve.wait_ge(rs_ready, 1)
            do(tt(newton2, rstd2, rstd2, ALU.mult))
            do(tt(newton2, newton2, veps2, ALU.mult))
            do(ts(newton2, newton2, -0.5, 1.5, ALU.mult, ALU.add))
            do(tt(rstd2, rstd2, newton2, ALU.mult))
            dve.wait_ge(zeroed, 16 * (TILES // NT))
            for t in range(NT):
                ts(y_all[:, t, :], x1_all[:, t, :], mv2[:, t, 0:1], rstd2[:, t:t + 1], ALU.subtract, ALU.mult).then_inc(y_ready, 1)
            for g in range(0, 8, 2):
                dve.wait_ge(yT_done, g + 1)
                nc.vector.tensor_copy(yT[g // 4][:, (g % 4) * BANK:(g % 4) * BANK + BANK], ht_ps[:, 0:BANK]).then_inc(yT_dve, 1)
            dve.wait_ge(lg_done, 1)
            dve.wait_ge(const_ready, 1)
            dve.wait_ge(wg_in, 32)

            def wide(v):
                return v.unsqueeze(2).to_broadcast([P, NT, E])

            def over_tiles(v):
                return v.unsqueeze(1).to_broadcast([P, NT, E])

            def largest(values, top, low, pick):
                do(red(out=top, in_=values, axis=AX.X, op=ALU.max))
                do(tt(equal, values, wide(top), ALU.is_equal))
                do(nc.vector.scalar_tensor_tensor(out=cand, in0=equal, scalar=-2.0 * E, in1=iota_e, op0=ALU.mult, op1=ALU.add))
                do(red(out=low, in_=cand, axis=AX.X, op=ALU.min))
                do(tt(pick, cand, wide(low), ALU.is_equal))

            do(tt(logits, lg_ps[:, 0:NT * E].rearrange("p (t e) -> p t e", e=E), over_tiles(bg_bc[:, :]), ALU.add))
            largest(logits, max1, min1, pick1)
            do(nc.vector.scalar_tensor_tensor(out=rest, in0=pick1, scalar=LOW, in1=logits, op0=ALU.mult, op1=ALU.add))
            largest(rest, max2, min1, pick2)
            tt(picks[:, :, :], pick1, pick2, ALU.add).then_inc(picked, 1)
            tt(diff, max2, max1, ALU.subtract).then_inc(diff_ready, 1)
            dve.wait_ge(ediff_ready, 1)
            do(ts(wt1, ediff, 1.0, None, ALU.add))
            do(nc.vector.reciprocal(wt1, wt1))
            do(tt(wt2, ediff, wt1, ALU.mult))
            do(nc.vector.memset(cum[:, 0, :], 0.0))
            dve.wait_ge(ranked, 1)
            for t in range(NT):
                do(tt(cum[:, t + 1, :], cum[:, t, :], y_ps[1][:, t * E:t * E + E], ALU.add))
            do(tt(tmp, cum[:, NT, :].unsqueeze(2).to_broadcast([P, E, NT]), iota_j, ALU.is_gt))
            do(red(out=tiles_e, in_=tmp, axis=AX.X, op=ALU.add))
            do(tt(tmp, tri, tiles_e.unsqueeze(1).to_broadcast([P, E, E]), ALU.mult))
            do(red(out=end_e, in_=tmp, axis=AX.X, op=ALU.add))
            do(tt(base_e, end_e, tiles_e, ALU.subtract))
            do(ts(base_e, base_e, float(P), None, ALU.mult))
            do(tt(pos, y_ps[0][:, 0:NT * E].rearrange("p (t e) -> p t e", e=E), cum[:, 0:NT, :], ALU.add))
            do(tt(pos, pos, over_tiles(base_e), ALU.add))
            for k, pick in enumerate((pick1, pick2)):
                do(tt(tmp, pos, pick, ALU.mult))
                do(red(out=slot_fp[:, k, :], in_=tmp, axis=AX.X, op=ALU.add))
            nc.vector.tensor_copy(slot_of[:, :, :], slot_fp[:, :, :]).then_inc(slots_ready, 1)
            do(tt(ended[:, :, :], end_e[0:1].unsqueeze(1).to_broadcast([1, TILES, E]), tile_iota[:, :, :], ALU.is_le))
            do(red(out=tile_expert[:, :], in_=ended[:, :, :], axis=AX.X, op=ALU.add))
            do(nc.vector.tensor_copy(tile_end_i[:, :], end_e[0:1]))
            ts(tile_expert_i[:, :], tile_expert[:, :], float(E - 1), None, ALU.min).then_inc(table_ready, 1)
            dve.wait_ge(table_ready, 1)
            dve.sem_inc(y_biased, 1)

            def x_low(t, i):
                dve.wait_ge(x_hi, t + 1)
                wait(dve, h_done, t - 1)
                tt(xT_lo[:, i, :], xt_ps[:, 0:DC * P], xT_hi[:, i, :].bitcast(F32), ALU.subtract).then_inc(x_lo, 1)

            def pair(phase, j):
                for i in range(2):
                    s = 2 * j + i
                    if has(phase, i, 0):
                        e = expert_of(dve, s)
                        dve.wait_ge(bias_ready, e + 1)
                        dve.wait_ge(h_done, s + 1)
                        wait(dve, ht_done, s - 1)
                        tt(hid[:, i, :], h_ps[:, :], b1_bc[:, bass.ds((e % 2) * HID, HID)], ALU.add).then_inc(h_biased, 1)
                    if has(phase, i, -1):
                        x_low(s + 1, 1 - i)
                    if has(phase, i, 1):
                        dve.wait_ge(h_hi, s)
                        wait(dve, y_done, s - 2)
                        tt(hT_lo[:, 1 - i, :], ht_ps[:, :], hT_hi[:, 1 - i, :].bitcast(F32), ALU.subtract).then_inc(h_lo, 1)
                    if has(phase, i, 2):
                        e = expert_of(dve, s - 2)
                        dve.wait_ge(y_done, s - 1)
                        wait(dve, sy_out[i], 16 * (j - 1))
                        tt(y_sb[:, i, :], y_ps[i][:, 0:D], b2_bc[:, bass.ds((e % 2) * D, D)], ALU.add).then_inc(y_biased, 1)

            x_low(0, 0)
            steps(dve, pair)
            for t in range(NT):
                dve.wait_ge(gathered[t % GB], 32 * (t // GB + 1))
                nc.vector.scalar_tensor_tensor(out=part[t % 2], in0=got[0][t % GB], scalar=wt1[:, t:t + 1], in1=x1_all[:, t, :],
                                               op0=ALU.mult, op1=ALU.add).then_inc(part_ready, 1)
                dve.wait_ge(part_ready, t + 1)
                if t >= 2:
                    dve.wait_ge(stored[t % 2], 16 * (t // 2))
                nc.vector.scalar_tensor_tensor(out=res[t % 2], in0=got[1][t % GB], scalar=wt2[:, t:t + 1], in1=part[t % 2],
                                               op0=ALU.mult, op1=ALU.add).then_inc(res_ready, 1)

        @block.tensor
        def _(pe):
            pe.wait_ge(const_ready, 1)
            for g in range(8):
                k, q = g // 4, g % 4
                pe.wait_ge(y_ready, 4 * q + 4)
                if g >= 2:
                    pe.wait_ge(yT_dve if g % 2 == 0 else yT_act, g // 2)
                for i in range(4):
                    last = nc.tensor.transpose(ht_ps[:, (g % 2) * BANK + i * P:(g % 2) * BANK + i * P + P],
                                               y_all[:, 4 * q + i, k * P:k * P + P], ident2[:, :])
                last.then_inc(yT_done, 1)
            pe.wait_ge(wg_in, 32)
            pe.wait_ge(yT_dve, 4)
            pe.wait_ge(yT_act, 4)
            for t in range(NT):
                for k in range(DC):
                    last = nc.tensor.matmul(lg_ps[:, t * E:t * E + E], yT[k][:, t * P:t * P + P], wg_sb[:, k, :],
                                            start=k == 0, stop=k == DC - 1)
            last.then_inc(lg_done, 1)
            pe.wait_ge(picked, 1)
            flat = picks[:, :, :].rearrange("p t e -> p (t e)")
            nc.tensor.matmul(y_ps[0][:, 0:NT * E], before[:, :], flat, start=True, stop=True)
            nc.tensor.matmul(y_ps[1][:, 0:NT * E], ones[:, :], flat, start=True, stop=True).then_inc(ranked, 1)
            pe.wait_ge(table_ready, 1)

            def transpose_rows(t, i, j):
                pe.wait_ge(sx_in[i], 16 * j + 16)
                wait(pe, x_lo, t)
                for k in range(DC):
                    last = nc.tensor.transpose(xt_ps[:, k * P:k * P + P], x_in_sb[:, i, k * P:k * P + P], ident2[:, :])
                last.then_inc(xt_done, 1)

            def up(t, i):
                e = expert_of(pe, t)
                base = (e % 2) * WC
                pe.wait_ge(w_ready, e + 1)
                wait(pe, h_biased, t)
                pe.wait_ge(x_lo, t + 1)
                for half in range(HID // BANK):
                    terms = [(x, w, k) for k in range(DC) for x, w in ((xT_hi, w_hi), (xT_hi, w_lo), (xT_lo, w_hi))]
                    for n_, (x, w, k) in enumerate(terms):
                        last = nc.tensor.matmul(h_ps[:, half * BANK:half * BANK + BANK], x[:, i, k * P:k * P + P],
                                                w[:, bass.ds(base + k * HID + half * BANK, BANK)],
                                                start=n_ == 0, stop=n_ == len(terms) - 1)
                last.then_inc(h_done, 1)

            def transpose_hidden(t, i):
                pe.wait_ge(gelu_done, t + 1)
                wait(pe, h_lo, t)
                for c in range(HC):
                    last = nc.tensor.transpose(ht_ps[:, c * P:c * P + P], hid[:, i, c:HID:HC], ident2[:, :])
                last.then_inc(ht_done, 1)

            def down(t, i):
                e = expert_of(pe, t)
                base = (e % 2) * WC + W1C
                pe.wait_ge(h_lo, t + 1)
                wait(pe, y_biased, t)
                for c in range(HC):
                    for n_, (x, w) in enumerate(((hT_hi, w_hi), (hT_hi, w_lo), (hT_lo, w_hi))):
                        last = nc.tensor.matmul(y_ps[i][:, 0:D], x[:, i, c * P:c * P + P], w[:, bass.ds(base + c * D, D)],
                                                start=c == 0 and n_ == 0, stop=c == HC - 1 and n_ == 2)
                last.then_inc(y_done, 1)

            def pair(phase, j):
                for i in range(2):
                    s = 2 * j + i
                    if has(phase, i, 0):
                        up(s, i)
                    if has(phase, i, -1):
                        transpose_rows(s + 1, 1 - i, j + i)
                    if has(phase, i, 1):
                        transpose_hidden(s - 1, 1 - i)
                    if has(phase, i, 2):
                        down(s - 2, i)

            transpose_rows(0, 0, 0)
            steps(pe, pair)


def layer(nc, x, adj, x2, v, wg, bg, w1, b1, w2, b2, out):
    P = 128
    N, D = x.shape
    E = w1.shape[0]
    tiles = -(-(N * 2 // P + E - 1) // (N // P)) * (N // P)
    x1 = nc.dram_tensor("x1", [N, D], F32).ap()
    slots_x = nc.dram_tensor("slots_x", [tiles * P, D], F32).ap()
    slots_y = nc.dram_tensor("slots_y", [tiles * P, D], F32).ap()
    graph_attention(nc, x, adj, x2, v, x1)
    expert_ffn(nc, x1, wg, bg, w1, b1, w2, b2, out, slots_x, slots_y)


_INS = ["x", "adj", "L0_gnn_x2", "L0_gnn_v", "L0_ffn_Wg", "L0_ffn_bg", "L0_ffn_W1", "L0_ffn_b1", "L0_ffn_W2", "L0_ffn_b2"]


def kernel(**inputs):
    import numpy as _np
    import concourse.bacc as _bacc
    from concourse import mybir as _mybir
    from concourse.bass_utils import run_bass_kernel_spmd as _run

    nc = _bacc.Bacc("TRN2", target_bir_lowering=False, num_devices=1)
    arrays, args = {}, []
    for name in _INS:
        a = _np.ascontiguousarray(inputs[name])
        arrays[f"in_{name}"] = a
        args.append(nc.dram_tensor(f"in_{name}", a.shape, _mybir.dt.from_np(a.dtype), kind="ExternalInput").ap())
    out = nc.dram_tensor("out", inputs["x"].shape, _mybir.dt.float32, kind="ExternalOutput").ap()
    layer(nc, *args, out)
    return _run(nc, [arrays], core_ids=[0]).results[0]["out"]
```

```python
from contextlib import ExitStack
import concourse.bass as bass
from concourse import mybir
F32, F32R, BF16, I32, U32 = mybir.dt.float32, mybir.dt.float32r, mybir.dt.bfloat16, mybir.dt.int32, mybir.dt.uint32
ALU = mybir.AluOpType
ACT = mybir.ActivationFunctionType
AX = mybir.AxisListType


def graph_attention(nc, x, adj, x2, v, x1, to_zero):
    N, D = x.shape
    H = 8
    DH = D // H
    P = 128
    NT = N // P
    KS = 3 * DH
    HALF = N // 2
    BANK = 512
    GRP = N // BANK
    BPG = BANK // P
    BATCH = 4
    SM = 4
    SCALE = DH ** -0.5
    MASKED = 9000000000000000.0
    EPS = 1e-5

    x_t = x.rearrange("(t p) d -> t p d", p=P)
    x_p = x.rearrange("(t p) d -> p t d", p=P)
    x2_p = x2.rearrange("(t p) d -> p t d", p=P)
    v_p = v.rearrange("(t p) d -> p t d", p=P)
    adj_t = adj.rearrange("(t p) m -> t p m", p=P)
    x1_t = x1.rearrange("(t p) d -> t p d", p=P)

    ctx = ExitStack()
    with ctx:
        def sb(name, shape, dt):
            return ctx.enter_context(nc.sbuf_tensor(name, shape, dt))

        def sem(name):
            return ctx.enter_context(nc.semaphore(name))

        keysT = sb("keysT", [KS, H, N], F32R)
        scores = sb("scores", [P, SM, N], F32)
        probsT = sb("probsT", [P, H, NT, P], F32)
        values = sb("values", [P, NT, D], F32)
        adj_bf = sb("adj_bf", [P, N], BF16)
        mask = sb("mask", [P, N], BF16)
        queriesT = sb("queriesT", [KS, H, P], F32R)
        q_nat = sb("q_nat", [P, H, 3, DH], F32R)
        x_q = sb("x_q", [P, D], F32)
        x_mid = sb("x_mid", [P, D], F32)
        xn = sb("xn", [P, D], F32)
        x_res = sb("x_res", [P, D], F32)
        att = sb("att", [P, D], F32)
        x1_sb = sb("x1_sb", [P, D], F32)
        outT = sb("outT", [P, 2, P], F32)
        ident = sb("ident", [P, P], F32)
        zeros = sb("zeros", [P, D], F32)
        row_min = sb("row_min", [P, 2, 4], F32)
        row_sum = sb("row_sum", [P, NT * H], F32)
        r_den = sb("r_den", [P, H], F32)
        stats = sb("stats", [P, NT, 6], F32)
        mean_var = sb("mean_var", [P, NT, 2], F32)
        veps = sb("veps", [P, NT], F32)
        rv = sb("rv", [P, NT], F32)
        rstd = sb("rstd", [P, NT], F32)
        newton = sb("newton", [P, NT], F32)
        nscale = sb("nscale", [P, NT], F32)
        x_all = probsT[:, 0:2, :, :].rearrange("p a t n -> p (a t n)").rearrange("p (t d) -> p t d", d=D)
        x2_all = scores[:, 0:2, :].rearrange("p a n -> p (a n)").rearrange("p (t d) -> p t d", d=D)
        k_nat = [scores[:, 2 + i, 0:H * KS].rearrange("p (h c d) -> p h c d", c=3, d=DH).bitcast(F32R) for i in range(2)]

        s_ps = [ctx.enter_context(nc.psum_tensor(f"s_ps{i}", [P, HALF], F32)) for i in range(2)]
        t_ps = [ctx.enter_context(nc.psum_tensor(f"t_ps{i}", [P, BANK], F32)) for i in range(2)]
        o_ps = ctx.enter_context(nc.psum_tensor("o_ps", [P, BANK], F32))
        a_ps = ctx.enter_context(nc.psum_tensor("a_ps", [P, BANK], F32))

        x_in, v_in, zeros_ready, zeroed = sem("x_in"), sem("v_in"), sem("zeros_ready"), sem("zeroed")
        x2_in = [sem(f"x2_in{i}") for i in range(4)]
        ident_zero, ident_ready = sem("ident_zero"), sem("ident_ready")
        k_hi, k_split, k_tr, k_ev = sem("k_hi"), sem("k_split"), sem("k_tr"), sem("k_ev")
        ln_step, rv_ready, rs_ready, ln_ready = sem("ln_step"), sem("rv_ready"), sem("rs_ready"), sem("ln_ready")
        adj_in, xq_in, xr_in, x1_out = sem("adj_in"), sem("xq_in"), sem("xr_in"), sem("x1_out")
        mask_done, dve_waited = sem("mask_done"), sem("dve_waited")
        xn_done, hi_done, q_split = sem("xn_done"), sem("hi_done"), sem("q_split")
        q_tr, q_ev = sem("q_tr"), sem("q_ev")
        s_done, first_min, row_ready, exp_done = sem("s_done"), sem("first_min"), sem("row_ready"), sem("exp_done")
        t_done, dve_ev, act_ev = sem("t_done"), sem("dve_ev"), sem("act_ev")
        pv_done, outT_ev, o_tr = sem("pv_done"), sem("outT_ev"), sem("o_tr")
        den_ready, att_ready, x1_ready = sem("den_ready"), sem("att_ready"), sem("x1_ready")

        DVE_GROUPS = [(0,), (0, 2)]
        ACT_GROUPS = [(1, 2, 3), (1, 3)]

        def copied(groups, it, h, g=GRP - 1):
            per = sum(len(groups[i % 2]) for i in range(H))
            return it * per + sum(len(groups[i % 2]) for i in range(h)) + sum(1 for i in groups[h % 2] if i <= g)

        FIRST, MID, LAST, DRAIN = range(4)

        def back(phase, it, h, d):
            if phase == FIRST and h < d or phase == DRAIN and h >= d:
                return None
            return (it, h - d) if h >= d else (it - 1, h - d + H)

        def wait(eng, s, value):
            if not isinstance(value, int) or value > 0:
                eng.wait_ge(s, value)

        def tiles(eng, step):
            step(FIRST, 0)
            step(MID, 1)
            with eng.Fori(2, NT - 1) as it:
                step(MID, it)
            step(LAST, NT - 1)
            step(DRAIN, NT)

        def key_tiles(eng, step, loaded=False):
            for c in range(4):
                if loaded:
                    eng.wait_ge(x2_in[c], 16)
                if c == 0:
                    step(0)
                with eng.Fori(max(2 * c, 1), 2 * c + 2) as j:
                    step(j)

        block = ctx.enter_context(nc.Block())

        @block.sync
        def _(sp):
            for i in range(4):
                sp.dma_start(x2_all[:, 4 * i:4 * i + 4, :], x2_p[:, 4 * i:4 * i + 4, :]).then_inc(x2_in[i], 16)
            sp.dma_start(x_all, x_p).then_inc(x_in, 16)
            sp.dma_start(x_q[:, :], x_t[0]).then_inc(xq_in, 16)
            sp.dma_start(values[:, :, :], v_p).then_inc(v_in, 16)

            sp.wait_ge(zeros_ready, 1)
            for table in to_zero:
                sp.dma_start(table.rearrange("(t p) d -> p t d", p=P),
                             zeros[:, :].unsqueeze(1).to_broadcast([P, table.shape[0] // P, D])).then_inc(zeroed, 16)

            def tile(phase, it):
                if phase in (FIRST, MID):
                    wait(sp, xn_done, it + 1)
                    sp.dma_start(x_q[:, :], x_t[it + 1]).then_inc(xq_in, 16)
                if phase != FIRST:
                    wait(sp, x1_ready, it - 1)
                    sp.dma_start(x_res[:, :], x_t[it - 1]).then_inc(xr_in, 16)
                    wait(sp, x1_ready, it)
                    sp.dma_start(x1_t[it - 1], x1_sb[:, :]).then_inc(x1_out, 16)

            tiles(sp, tile)
            sp.wait_ge(x1_out, 16 * NT)
            sp.wait_ge(zeroed, 16 * len(to_zero))

        @block.gpsimd
        def _(pool):
            pool.dma_start(adj_bf[:, :], adj_t[0]).then_inc(adj_in, 16)
            nc.gpsimd.memset(ident[:, :], 0.0).then_inc(ident_zero, 1)
            nc.gpsimd.memset(zeros[:, :], 0.0).then_inc(zeros_ready, 1)
            pool.wait_ge(ident_zero, 1)
            nc.gpsimd.affine_select(out=ident[:, :], in_=ident[:, :], compare_op=ALU.not_equal, fill=1.0, base=0,
                                    pattern=[[-1, P]], channel_multiplier=1).then_inc(ident_ready, 1)

            def key_lows(j):
                for i in range(2):
                    t = 2 * j + i
                    wait(pool, k_hi, 2 * t + 2)
                    nc.gpsimd.tensor_tensor(out=k_nat[i][:, :, 1, :],
                                            in0=x2_all[:, bass.ds(t, 1), :].rearrange("p a (h d) -> p (a h) d", d=DH),
                                            in1=k_nat[i][:, :, 0, :].bitcast(F32), op=ALU.subtract).then_inc(k_split, 1)

            key_tiles(pool, key_lows, loaded=True)

            def split_queries(t):
                wait(pool, xq_in, 16 * t + 16)
                if isinstance(t, int) and t == 0:
                    pool.wait_ge(ln_ready, 1)
                wait(pool, q_split, t)
                row = [P, D]
                nc.gpsimd.tensor_tensor(out=x_mid[:, :], in0=x_q[:, :], in1=mean_var[:, bass.ds(t, 1), 0].to_broadcast(row),
                                        op=ALU.subtract).then_inc(xn_done, 1)
                wait(pool, xn_done, t + 1)
                wait(pool, q_tr, 2 * t)
                scale = nscale[:, bass.ds(t, 1)].to_broadcast(row)
                nc.gpsimd.tensor_tensor(out=xn[:, :], in0=x_mid[:, :], in1=scale, op=ALU.mult)
                for c in range(2):
                    nc.gpsimd.tensor_tensor(out=q_nat[:, :, c, :], in0=x_mid[:, :].rearrange("p (h d) -> p h d", d=DH),
                                            in1=nscale[:, bass.ds(t, 1)].unsqueeze(2).to_broadcast([P, H, DH]),
                                            op=ALU.mult).then_inc(hi_done, 1)
                wait(pool, hi_done, 2 * t + 2)
                nc.gpsimd.tensor_tensor(out=q_nat[:, :, 2, :], in0=xn[:, :].rearrange("p (h d) -> p h d", d=DH),
                                        in1=q_nat[:, :, 0, :].bitcast(F32), op=ALU.subtract).then_inc(q_split, 1)

            split_queries(0)

            def tile(phase, it):
                if phase in (FIRST, MID):
                    wait(pool, mask_done, it + 1)
                    pool.dma_start(adj_bf[:, :], adj_t[it + 1]).then_inc(adj_in, 16)
                    split_queries(it + 1)
                if phase != FIRST:
                    wait(pool, xr_in, 16 * it)
                    wait(pool, att_ready, it)
                    wait(pool, x1_out, 16 * (it - 1))
                    nc.gpsimd.tensor_tensor(out=x1_sb[:, :], in0=att[:, :], in1=x_res[:, :], op=ALU.add).then_inc(x1_ready, 1)

            tiles(pool, tile)

        @block.scalar
        def _(act):
            def key_highs(j):
                for i in range(2):
                    t = 2 * j + i
                    wait(act, k_tr, t - 1)
                    for c in (0, 2):
                        nc.scalar.copy(k_nat[i][:, :, c, :],
                                       x2_all[:, bass.ds(t, 1), :].rearrange("p a (h d) -> p (a h) d", d=DH)).then_inc(k_hi, 1)

            key_tiles(act, key_highs, loaded=True)
            act.wait_ge(rv_ready, 1)
            nc.scalar.activation(rstd[:, :], rv[:, :], ACT.Sqrt).then_inc(rs_ready, 1)

            def copy_queries(t, half):
                wait(act, q_tr, 2 * t + half + 1)
                wait(act, s_done, 2 * (H * (t - 1) + BATCH * half + BATCH))
                nc.scalar.copy(queriesT[:, BATCH * half:BATCH * half + BATCH, :],
                               a_ps[0:KS, :].rearrange("p (h n) -> p h n", n=P)).then_inc(q_ev, 1)

            copy_queries(0, 0)

            def tile(phase, it):
                for h in range(H):
                    if phase in (FIRST, MID, LAST) and h == 0:
                        copy_queries(it, 1)
                    two = back(phase, it, h, 2)
                    if two is not None:
                        copy_group(*two, 1)
                    prev = back(phase, it, h, 1)
                    if prev is not None:
                        t, g = prev
                        wait(act, row_ready, H * t + g + 1)
                        buf = scores[:, g % SM, :]
                        nc.scalar.activation(buf, buf, ACT.Exp, bias=row_min[:, 1, g % 4:g % 4 + 1], scale=-1.0,
                                             accum_out=row_sum[:, bass.ds(t * H + g, 1)]).then_inc(exp_done, 1)
                    if two is not None:
                        for grp in ACT_GROUPS[two[1] % 2][1:]:
                            copy_group(*two, grp)
                    if phase in (FIRST, MID) and h == 4:
                        copy_queries(it + 1, 0)

            def copy_group(t, g, grp):
                wait(act, t_done, GRP * (H * t + g) + grp + 1)
                if not (isinstance(t, int) and t == 0):
                    act.wait_ge(pv_done, 2 * t - 1 + g // BATCH)
                nc.scalar.copy(probsT[:, g, BPG * grp:BPG * grp + BPG, :],
                               t_ps[grp % 2][:, :].rearrange("p (c n) -> p c n", n=P)).then_inc(act_ev, 1)

            tiles(act, tile)

        @block.vector
        def _(dve):
            n_ln = [0]

            def ln(ins):
                n_ln[0] += 1
                ins.then_inc(ln_step, 1)
                dve.wait_ge(ln_step, n_ln[0])

            dve.wait_ge(x_in, 16)
            for t in range(NT):
                last = nc.vector.bn_stats(out=stats[:, t, :], in_=x_all[:, t, :])
            ln(last)
            for t in range(NT):
                last = nc.vector.bn_aggr(out=mean_var[:, t, :], in_=stats[:, t, :])
            ln(last)
            ln(nc.vector.tensor_scalar(veps[:, :], mean_var[:, :, 1], EPS, None, ALU.add))
            ln(nc.vector.reciprocal(rv[:, :], veps[:, :]))
            nc.vector.tensor_scalar(rv[:, :], rv[:, :], 1.0, None, ALU.mult).then_inc(rv_ready, 1)

            def copy_keys(j):
                for i in range(2):
                    t = 2 * j + i
                    dve.wait_ge(k_tr, t + 1)
                    nc.vector.tensor_copy(out=keysT[:, :, bass.ds(t * P, P)],
                                          in_=s_ps[i][0:KS, :].rearrange("p (h n) -> p h n", n=P)).then_inc(k_ev, 1)

            key_tiles(dve, copy_keys)
            dve.wait_ge(rs_ready, 1)
            ln(nc.vector.tensor_tensor(newton[:, :], rstd[:, :], rstd[:, :], ALU.mult))
            ln(nc.vector.tensor_tensor(newton[:, :], newton[:, :], veps[:, :], ALU.mult))
            ln(nc.vector.tensor_scalar(newton[:, :], newton[:, :], -0.5, 1.5, ALU.mult, ALU.add))
            ln(nc.vector.tensor_tensor(rstd[:, :], rstd[:, :], newton[:, :], ALU.mult))
            nc.vector.tensor_scalar(nscale[:, :], rstd[:, :], -SCALE, None, ALU.mult).then_inc(ln_ready, 1)

            def slot_free(eng, t, g):
                if not (isinstance(t, int) and t == 0):
                    eng.wait_ge(pv_done, 2 * t - 1 + g // BATCH)

            def tile(phase, it):
                for h in range(H):
                    u = H * it + h
                    if phase != DRAIN:
                        if h == 0:
                            dve.wait_ge(adj_in, 16 * it + 16)
                            wait(dve, row_ready, u)
                            nc.vector.tensor_scalar(mask[:, :], adj_bf[:, :], 0.0, MASKED, ALU.is_le,
                                                    ALU.mult).then_inc(mask_done, 1)
                            dve.wait_ge(mask_done, it + 1)
                        dve.wait_ge(s_done, 2 * u + 1)
                        if back(phase, it, h, SM) is not None:
                            dve.wait_ge(t_done, GRP * (u - SM) + GRP)
                        dve.sem_inc(dve_waited, 1)
                        nc.vector.tensor_tensor_reduce(
                            out=scores[:, h % SM, 0:HALF], in0=s_ps[0][:, :], in1=mask[:, 0:HALF], scale=1.0, scalar=3e38,
                            op0=ALU.add, op1=ALU.min, accum_out=row_min[:, 0, h % 4:h % 4 + 1]).then_inc(first_min, 1)
                    prev = back(phase, it, h, 2)
                    if prev is not None:
                        t, g = prev
                        slot_free(dve, t, g)
                        for grp in DVE_GROUPS[g % 2]:
                            if grp:
                                continue
                            dve.wait_ge(t_done, GRP * (H * t + g) + grp + 1)
                            nc.vector.tensor_copy(out=probsT[:, g, BPG * grp:BPG * grp + BPG, :],
                                                  in_=t_ps[grp % 2][:, :].rearrange("p (c n) -> p c n", n=P)).then_inc(dve_ev, 1)
                    if phase != DRAIN:
                        dve.wait_ge(s_done, 2 * u + 2)
                        dve.wait_ge(first_min, u + 1)
                        dve.sem_inc(dve_waited, 1)
                        dve.sem_inc(dve_waited, 1)
                        nc.vector.tensor_tensor_reduce(
                            out=scores[:, h % SM, HALF:N], in0=s_ps[1][:, :], in1=mask[:, HALF:N], scale=1.0,
                            scalar=row_min[:, 0, h % 4:h % 4 + 1], op0=ALU.add, op1=ALU.min,
                            accum_out=row_min[:, 1, h % 4:h % 4 + 1]).then_inc(row_ready, 1)
                    if prev is not None:
                        for grp in DVE_GROUPS[g % 2]:
                            if not grp:
                                continue
                            dve.wait_ge(t_done, GRP * (H * t + g) + grp + 1)
                            nc.vector.tensor_copy(out=probsT[:, g, BPG * grp:BPG * grp + BPG, :],
                                                  in_=t_ps[grp % 2][:, :].rearrange("p (c n) -> p c n", n=P)).then_inc(dve_ev, 1)
                    if phase != FIRST and h in (2, 6):
                        b = 2 * it - 2 + h // BATCH
                        dve.wait_ge(pv_done, b + 1)
                        wait(dve, o_tr, it - 1)
                        nc.vector.tensor_copy(out=outT[:, h // BATCH, :], in_=o_ps[:, 0:P]).then_inc(outT_ev, 1)
                    if phase != FIRST and h == 7:
                        dve.wait_ge(exp_done, H * it)
                        wait(dve, att_ready, it - 1)
                        nc.vector.reciprocal(r_den[:, :], row_sum[:, bass.ds((it - 1) * H, H)]).then_inc(den_ready, 1)
                        dve.wait_ge(den_ready, it)
                        dve.wait_ge(o_tr, it)
                        wait(dve, x1_ready, it - 1)
                        nc.vector.tensor_tensor(att[:, :].rearrange("p (h d) -> p h d", d=DH),
                                                a_ps[:, 0:D].rearrange("p (h d) -> p h d", d=DH),
                                                r_den[:, :].unsqueeze(2).to_broadcast([P, H, DH]), ALU.mult).then_inc(att_ready, 1)

            tiles(dve, tile)

        @block.tensor
        def _(pe):
            pe.wait_ge(ident_ready, 1)

            def transpose_keys(j):
                for i in range(2):
                    t = 2 * j + i
                    pe.wait_ge(k_split, t + 1)
                    pe.wait_ge(k_hi, 2 * t + 2)
                    wait(pe, k_ev, t - 1)
                    for h in range(H):
                        last = nc.tensor.transpose(s_ps[i][0:KS, h * P:h * P + P],
                                                   k_nat[i][:, h, :, :].bitcast(F32).rearrange("p c d -> p (c d)"), ident[:, :])
                    last.then_inc(k_tr, 1)

            key_tiles(pe, transpose_keys)

            def transpose_queries(t, half):
                pe.wait_ge(q_split, t + 1)
                pe.wait_ge(hi_done, 2 * t + 2)
                if half == 0:
                    wait(pe, q_ev, 2 * t)
                else:
                    wait(pe, att_ready, t - 1)
                    pe.wait_ge(q_ev, 2 * t + 1)
                for i in range(BATCH):
                    last = nc.tensor.transpose(a_ps[0:KS, i * P:i * P + P],
                                               q_nat[:, BATCH * half + i, :, :].bitcast(F32).rearrange("p c d -> p (c d)"),
                                               ident[:, :])
                last.then_inc(q_tr, 1)

            def score(t, h, half):
                u = H * t + h
                if half == 0:
                    pe.wait_ge(q_ev, 2 * t + 1 + h // BATCH)
                    wait(pe, first_min, u)
                    if isinstance(t, int) and t == 0:
                        pe.wait_ge(k_ev, NT)
                else:
                    wait(pe, row_ready, u)
                for c in range(HALF // BANK):
                    m = half * HALF + c * BANK
                    last = nc.tensor.matmul(s_ps[half][:, c * BANK:c * BANK + BANK], queriesT[:, h, :], keysT[:, h, m:m + BANK],
                                            start=True, stop=True)
                last.then_inc(s_done, 1)

            def transpose_probs(t, h, grp):
                u = H * t + h
                if grp == 0:
                    pe.wait_ge(exp_done, u + 1)
                before = (t, h, grp - 2) if grp >= 2 else (t, h - 1, grp + 2) if h else (t - 1, H - 1, grp + 2)
                tt, hh, gg = before
                if gg in DVE_GROUPS[hh % 2]:
                    wait(pe, dve_ev, copied(DVE_GROUPS, tt, hh, gg))
                else:
                    wait(pe, act_ev, copied(ACT_GROUPS, tt, hh, gg))
                for i in range(BPG):
                    m = (grp * BPG + i) * P
                    last = nc.tensor.transpose(t_ps[grp % 2][:, i * P:i * P + P], scores[:, h % SM, m:m + P], ident[:, :])
                last.then_inc(t_done, 1)

            def value_products(t, half, quarter):
                if quarter == 0:
                    hh = BATCH * half + BATCH - 1
                    pe.wait_ge(dve_ev, copied(DVE_GROUPS, t, hh))
                    pe.wait_ge(act_ev, copied(ACT_GROUPS, t, hh))
                    wait(pe, outT_ev, 2 * t + half)
                    if isinstance(t, int) and t == 0:
                        pe.wait_ge(v_in, 16)
                for c in range(BPG * quarter, BPG * quarter + BPG):
                    for i in range(BATCH):
                        h = BATCH * half + i
                        last = nc.tensor.matmul(o_ps[DH * i:DH * i + DH, 0:P], values[:, c, h * DH:h * DH + DH],
                                                probsT[:, h, c, :], start=c == 0, stop=c == NT - 1,
                                                tile_position=(0, DH * i))
                if quarter == GRP - 1:
                    last.then_inc(pv_done, 1)

            def transpose_out(phase, t):
                pe.wait_ge(outT_ev, 2 * t + 2)
                pe.wait_ge(q_ev, 2 * NT if phase in (LAST, DRAIN) else 2 * t + 5)
                for half in range(2):
                    last = nc.tensor.transpose(a_ps[:, half * P:half * P + P], outT[:, half, :], ident[:, :])
                last.then_inc(o_tr, 1)

            transpose_queries(0, 0)
            score(0, 0, 0)
            score(0, 0, 1)

            def tile(phase, it):
                for h in range(H):
                    if phase != DRAIN and h == 0:
                        transpose_queries(it, 1)
                    ahead = phase in (FIRST, MID) or phase == LAST and h < H - 1
                    nxt = (it, h + 1) if h < H - 1 else (it + 1, 0)
                    prev = back(phase, it, h, 2)
                    if prev is not None:
                        transpose_probs(*prev, 0)
                        transpose_probs(*prev, 1)
                    if ahead:
                        score(*nxt, 0)
                    if prev is not None:
                        transpose_probs(*prev, 2)
                        transpose_probs(*prev, 3)
                    if phase == DRAIN and h < 6 or phase == MID or phase == LAST or phase == FIRST and h >= 6:
                        t, half = (it, 0) if h >= 6 else (it - 1, 0 if h < 2 else 1)
                        value_products(t, half, (h - 6) % 4)
                    if ahead:
                        score(*nxt, 1)
                    if phase in (FIRST, MID) and h == 4:
                        transpose_queries(it + 1, 0)
                    if phase != FIRST and h == 7:
                        transpose_out(phase, it - 1)

            tiles(pe, tile)


def expert_ffn(nc, x1, wg, bg, w1, b1, w2, b2, out, slots_x, slots_y):
    N, D = x1.shape
    E, _, HID = w1.shape
    P = 128
    NT = N // P
    TOPK = 2
    DC = D // P
    HC = HID // P
    BANK = 512
    TILES = slots_x.shape[0] // P
    assert TILES >= N * TOPK // P + E - 1 and TILES % 2 == 0 and N // P <= E
    FEWEST = N * TOPK // P // 2
    EPS = 1e-5
    LOW = -3e38
    W1C, W2C = DC * HID, HC * D
    WC = W1C + W2C

    x1_p = x1.rearrange("(t p) d -> p t d", p=P)
    out_t = out.rearrange("(t p) d -> t p d", p=P)
    wg_p = wg.rearrange("(k p) e -> p k e", p=P)
    w1_p = w1.rearrange("e (k p) h -> e p k h", p=P)
    w2_p = w2.rearrange("e (p c) d -> e p (c d)", c=HC)
    sx_t = slots_x.rearrange("(i p) d -> i p d", p=P)
    sy_t = slots_y.rearrange("(i p) d -> i p d", p=P)

    ctx = ExitStack()
    with ctx:
        def sb(name, shape, dt):
            return ctx.enter_context(nc.sbuf_tensor(name, shape, dt))

        def sem(name):
            return ctx.enter_context(nc.semaphore(name))

        w_raw = sb("w_raw", [P, 2, WC], F32)
        w_hi = sb("w_hi", [P, 2 * WC], F32R)
        w_lo = sb("w_lo", [P, 2 * WC], F32R)
        b1_bc = sb("b1_bc", [P, 2 * HID], F32)
        b2_bc = sb("b2_bc", [P, 2 * D], F32)
        x1_all = sb("x1_all", [P, NT, D], F32)
        y_all = sb("y_all", [P, NT, D], F32)
        ident2 = sb("ident2", [P, P], F32)
        route = sb("route", [P, 16, NT, E], F32)
        small = sb("small", [P, 12, NT], F32)
        picks = sb("picks", [P, NT, E], BF16)
        before = sb("before", [P, P], BF16)
        ones = sb("ones", [P, P], BF16)
        wg_sb = sb("wg_sb", [P, DC, E], F32)
        bg_bc = sb("bg_bc", [P, E], F32)
        cum = sb("cum", [P, NT + 1, E], F32)
        slot_fp = sb("slot_fp", [P, TOPK, NT], F32)
        slot_of = sb("slot_of", [P, TOPK, NT], U32)
        tile_iota = sb("tile_iota", [1, TILES, E], F32)
        ended = sb("ended", [1, TILES, E], F32)
        tile_expert = sb("tile_expert", [1, TILES], F32)
        tile_expert_i = sb("tile_expert_i", [1, TILES], I32)
        tile_end_i = sb("tile_end_i", [1, E], I32)
        over_pairs = sb("over_pairs", [1, TILES // 2], F32)
        n_pairs = sb("n_pairs", [1, 1], F32)
        n_pairs_i = sb("n_pairs_i", [1, 1], I32)
        stats2 = sb("stats2", [P, NT, 6], F32)
        mv2 = sb("mv2", [P, NT, 2], F32)
        x_in_sb = sb("x_in_sb", [P, 2, D], F32)
        xT_hi = sb("xT_hi", [P, 2, DC * P], F32R)
        xT_lo = sb("xT_lo", [P, 2, DC * P], F32R)
        hid = sb("hid", [P, 2, HID], F32)
        hT_hi = sb("hT_hi", [P, 2, HID], F32R)
        hT_lo = sb("hT_lo", [P, 2, HID], F32R)
        y_sb = sb("y_sb", [P, 2, D], F32)
        yT = [hid[:, :, :].rearrange("p a h -> p (a h)"), sb("yT_second", [P, N], F32)[:, :]]
        got = [[w_raw[:, k, i * D:i * D + D] for i in range(NT)] for k in range(TOPK)]
        res = [hid[:, 0, i * D:i * D + D] for i in range(2)]
        part = [hid[:, 1, i * D:i * D + D] for i in range(2)]

        logits, equal, cand, pick1, rest, pick2, pos, tmp, iota_e, iota_j, tri, zero = (route[:, i] for i in range(12))
        tiles_e, end_e, base_e = (route[:, 12, i, :] for i in range(3))
        max1, min1, max2, diff, ediff, wt1, wt2, veps2, rv2, rstd2, newton2, mean_n = (small[:, i, :] for i in range(12))

        h_ps = ctx.enter_context(nc.psum_tensor("h_ps", [P, HID], F32))
        ht_ps = ctx.enter_context(nc.psum_tensor("ht_ps", [P, HID], F32))
        y_ps = [ctx.enter_context(nc.psum_tensor(f"y_ps{i}", [P, BANK], F32)) for i in range(2)]
        xt_ps = ctx.enter_context(nc.psum_tensor("xt_ps", [P, BANK], F32))
        lg_ps = ctx.enter_context(nc.psum_tensor("lg_ps", [P, BANK], F32))

        x1_in, wg_in = sem("x1_in"), sem("wg_in")
        const_step, const_ready = sem("const_step"), sem("const_ready")
        step, rv_ready, rs_ready = sem("step"), sem("rv2_ready"), sem("rs2_ready")
        y_ready, yT_done, yT_dve, yT_act, lg_done = sem("y_ready"), sem("yT_done"), sem("yT_dve"), sem("yT_act"), sem("lg_done")
        picked, ranked, diff_ready, ediff_ready = sem("picked"), sem("ranked"), sem("diff_ready"), sem("ediff_ready")
        slots_ready, table_ready, scattered = sem("slots_ready"), sem("table_ready"), sem("scattered")
        w1_in, w2_in, b1_in, b2_in = ([sem(f"{n}_in{i}") for i in range(2)] for n in ("w1", "w2", "b1", "b2"))
        pool_waited = sem("pool_waited")
        hi_ready = [sem("w1_hi_ready"), sem("w2_hi_ready")]
        w1_ready, w2_ready = sem("w1_ready"), sem("w2_ready")
        sx_in = [sem(f"sx_in{i}") for i in range(2)]
        xt_done, x_hi, x_lo = sem("xt_done"), sem("x_hi"), sem("x_lo")
        h_done, h_biased, gelu_done = sem("h_done"), sem("h_biased"), sem("gelu_done")
        ht_done, h_hi, h_lo = sem("ht_done"), sem("h_hi"), sem("h_lo")
        y_done, y_biased = sem("y_done"), sem("y_biased")
        sy_out = [sem(f"sy_out{i}") for i in range(2)]
        gathered = [sem(f"gathered{i}") for i in range(NT)]
        part_ready, res_ready = sem("part_ready"), sem("res_ready")
        stored = [sem(f"stored{i}") for i in range(2)]

        def wait(eng, s, value):
            if not isinstance(value, int) or value > 0:
                eng.wait_ge(s, value)

        def pairs_of(eng):
            return eng.value_load(n_pairs_i[0:1, 0:1], min_val=0, max_val=TILES // 2 - FEWEST) + FEWEST

        def steps(eng, pair):
            pair(0, 0)
            pair(1, 1)
            pairs = pairs_of(eng)
            with eng.Fori(2, TILES // 2 - 1) as j:
                with eng.If(j < pairs - 1):
                    pair(1, j)
            pairs = pairs_of(eng)
            pair(2, pairs - 1)
            pair(3, pairs)

        def has(phase, i, d):
            if phase == 0:
                return i >= d
            if phase == 2:
                return i - d < 2
            if phase == 3:
                return i - d < 0
            return True

        def expert_of(eng, tile):
            return eng.value_load(tile_expert_i[0:1, bass.ds(tile, 1)], min_val=0, max_val=E - 1)

        block = ctx.enter_context(nc.Block())

        @block.sync
        def _(sp):
            def later(e):
                return not isinstance(e, int) or e >= 2

            def load_up(e, i):
                if later(e):
                    sp.wait_ge(w1_ready, e - 1)
                sp.dma_start(w_raw[:, i, 0:W1C].rearrange("p (k h) -> p k h", k=DC),
                             w1_p[bass.ds(e, 1)].rearrange("a p k h -> p (a k) h")).then_inc(w1_in[i], 16)

            def load_down(e, i):
                if later(e):
                    sp.wait_ge(w2_ready, e - 1)
                sp.dma_start(w_raw[:, i, W1C:WC], w2_p[bass.ds(e, 1)].rearrange("a p n -> p (a n)")).then_inc(w2_in[i], 16)

            def load_bias(e, i, src, dst, width, used, into):
                if later(e):
                    done = sp.value_load(tile_end_i[0:1, bass.ds(e - 2, 1)], min_val=1, max_val=TILES)
                    sp.wait_ge(used, done)
                sp.dma_start(dst[:, i * width:i * width + width], src[bass.ds(e, 1), :].to_broadcast([P, width])
                             ).then_inc(into[i], 16)

            def load_up_bias(e, i):
                load_bias(e, i, b1, b1_bc, HID, h_biased, b1_in)

            def load_down_bias(e, i):
                load_bias(e, i, b2, b2_bc, D, y_biased, b2_in)

            sp.dma_start(x1_all[:, :, :], x1_p).then_inc(x1_in, 16)
            sp.dma_start(wg_sb[:, :, :], wg_p).then_inc(wg_in, 16)
            sp.dma_start(bg_bc[:, :], bg.rearrange("(a e) -> a e", a=1).to_broadcast([P, E])).then_inc(wg_in, 16)
            for load in (load_up, load_down, load_up_bias, load_down_bias):
                for i in range(2):
                    load(i, i)
            sp.wait_ge(table_ready, 1)

            load_up(2, 0)
            load_up(3, 1)
            load_down(2, 0)
            load_up_bias(2, 0)
            with sp.Fori(2, E // 2) as j:
                for i in range(2):
                    load_up(2 * j + i, i)
                    load_down(2 * j + i - 1, 1 - i)
                    load_up_bias(2 * j + i - 1, 1 - i)
                    load_down_bias(2 * j + i - 2, i)
            load_down(E - 1, 1)
            load_up_bias(E - 1, 1)
            load_down_bias(E - 2, 0)
            load_down_bias(E - 1, 1)
            for t in range(NT):
                sp.wait_ge(res_ready, t + 1)
                sp.dma_start(out_t[t], res[t % 2]).then_inc(stored[t % 2], 16)
            for i in range(2):
                sp.wait_ge(stored[i], 16 * NT // 2)

        @block.gpsimd
        def _(pool):
            n_c = [0]

            def const(ins):
                n_c[0] += 1
                ins.then_inc(const_step, 1)
                pool.wait_ge(const_step, n_c[0])

            const(nc.gpsimd.memset(ident2[:, :], 0.0))
            nc.gpsimd.affine_select(out=ident2[:, :], in_=ident2[:, :], compare_op=ALU.not_equal, fill=1.0, base=0,
                                    pattern=[[-1, P]], channel_multiplier=1)
            nc.gpsimd.memset(ones[:, :], 1.0)
            const(nc.gpsimd.memset(before[:, :], 1.0))
            nc.gpsimd.affine_select(out=before[:, :], in_=before[:, :], compare_op=ALU.is_gt, fill=0.0, base=0,
                                    pattern=[[1, P]], channel_multiplier=-1)
            nc.gpsimd.iota(iota_e, pattern=[[0, NT], [1, E]], base=0, channel_multiplier=0, allow_small_or_imprecise_dtypes=True)
            nc.gpsimd.iota(iota_j, pattern=[[0, E], [P, NT]], base=0, channel_multiplier=0, allow_small_or_imprecise_dtypes=True)
            nc.gpsimd.iota(tile_iota[:, :, :], pattern=[[1, TILES], [0, E]], base=0, channel_multiplier=0,
                           allow_small_or_imprecise_dtypes=True)
            const(nc.gpsimd.memset(tri, 1.0))
            nc.gpsimd.affine_select(out=tri, in_=tri, compare_op=ALU.is_ge, fill=0.0, base=0,
                                    pattern=[[1, E], [-1, E]], channel_multiplier=0).then_inc(const_ready, 1)

            pool.wait_ge(slots_ready, 1)
            pool.wait_ge(y_ready, NT)
            for k in range(TOPK):
                for t in range(NT):
                    pool.indirect_dma_start(out=slots_x[:, :], out_offset=bass.IndirectOffsetOnAxis(ap=slot_of[:, k, t:t + 1], axis=0),
                                            in_=y_all[:, t, :], in_offset=None).then_inc(scattered, 16)
            pool.wait_ge(table_ready, 1)

            def split(e, i, j, second):
                at, to, w_in, b_in, used, ready = ((0, W1C, w1_in, b1_in, h_done, w1_ready),
                                                   (W1C, WC, w2_in, b2_in, y_done, w2_ready))[second]
                if not isinstance(e, int) or e >= 2:
                    done = pool.value_load(tile_end_i[0:1, bass.ds(e - 2, 1)], min_val=1, max_val=TILES)
                    pool.wait_ge(used, done)
                pool.wait_ge(w_in[i], 16 * j + 16)
                pool.sem_inc(pool_waited, 1)
                high, low = w_hi[:, i * WC + at:i * WC + to], w_lo[:, i * WC + at:i * WC + to]
                nc.gpsimd.tensor_scalar(high, w_raw[:, i, at:to], 1.0, 0.0, ALU.mult, ALU.add).then_inc(hi_ready[second], 1)
                pool.wait_ge(hi_ready[second], e + 1)
                pool.wait_ge(b_in[i], 16 * j + 16)
                pool.sem_inc(pool_waited, 1)
                nc.gpsimd.tensor_tensor(out=low, in0=w_raw[:, i, at:to], in1=high.bitcast(F32),
                                        op=ALU.subtract).then_inc(ready, 1)

            split(0, 0, 0, False)
            split(1, 1, 0, False)
            split(0, 0, 0, True)
            split(2, 0, 1, False)
            split(1, 1, 0, True)
            split(3, 1, 1, False)
            split(2, 0, 1, True)
            with pool.Fori(2, E // 2) as j:
                split(2 * j, 0, j, False)
                split(2 * j - 1, 1, j - 1, True)
                split(2 * j + 1, 1, j, False)
                split(2 * j, 0, j, True)
            split(E - 1, 1, E // 2 - 1, True)

            pairs = pairs_of(pool)
            for i in range(2):
                pool.wait_ge(sy_out[i], 16 * pairs)
            pool.sem_inc(pool_waited, 1)
            for t in range(NT):
                for k in range(TOPK):
                    pool.indirect_dma_start(out=got[k][t], out_offset=None, in_=slots_y[:, :],
                                            in_offset=bass.IndirectOffsetOnAxis(ap=slot_of[:, k, t:t + 1], axis=0)
                                            ).then_inc(gathered[t], 16)

        @block.scalar
        def _(act):
            act.wait_ge(rv_ready, 1)
            nc.scalar.activation(rstd2, rv2, ACT.Sqrt).then_inc(rs_ready, 1)
            for g in range(1, 8, 2):
                act.wait_ge(yT_done, g + 1)
                nc.scalar.copy(yT[g // 4][:, (g % 4) * BANK:(g % 4) * BANK + BANK], ht_ps[:, BANK:2 * BANK]).then_inc(yT_act, 1)
            act.wait_ge(diff_ready, 1)
            nc.scalar.activation(ediff, diff, ACT.Exp).then_inc(ediff_ready, 1)

            def pair(phase, j):
                for i in range(2):
                    s = 2 * j + i
                    if has(phase, i, 0):
                        if has(phase, i, -2):
                            act.wait_ge(xt_done, s + 1)
                            load_rows(s + 2, i)
                        act.wait_ge(h_biased, s + 1)
                        nc.scalar.activation(hid[:, i, :], hid[:, i, :], ACT.Gelu).then_inc(gelu_done, 1)
                    if has(phase, i, -1):
                        x_high(s + 1, 1 - i)
                    if has(phase, i, 1):
                        act.wait_ge(ht_done, s)
                        wait(act, y_done, s - 2)
                        nc.scalar.copy(hT_hi[:, 1 - i, :], ht_ps[:, :]).then_inc(h_hi, 1)
                    if has(phase, i, 2):
                        act.wait_ge(y_biased, s - 1)
                        act.dma_start(sy_t[s - 2], y_sb[:, i, :]).then_inc(sy_out[i], 16)

            def load_rows(t, i):
                act.dma_start(x_in_sb[:, i, :], sx_t[t]).then_inc(sx_in[i], 16)

            def x_high(t, i):
                act.wait_ge(xt_done, t + 1)
                wait(act, h_done, t - 1)
                nc.scalar.copy(xT_hi[:, i, :], xt_ps[:, 0:DC * P]).then_inc(x_hi, 1)

            act.wait_ge(scattered, 16 * TOPK * NT)
            for i in range(2):
                load_rows(i, i)
            x_high(0, 0)
            steps(act, pair)

        @block.vector
        def _(dve):
            n = [0]

            def do(ins):
                n[0] += 1
                ins.then_inc(step, 1)
                dve.wait_ge(step, n[0])

            tt, ts, red = nc.vector.tensor_tensor, nc.vector.tensor_scalar, nc.vector.tensor_reduce
            dve.wait_ge(x1_in, 16)
            for t in range(NT):
                last = nc.vector.bn_stats(out=stats2[:, t, :], in_=x1_all[:, t, :])
            do(last)
            for t in range(NT):
                last = nc.vector.bn_aggr(out=mv2[:, t, :], in_=stats2[:, t, :])
            do(last)
            do(ts(veps2, mv2[:, :, 1], EPS, None, ALU.add))
            nc.vector.reciprocal(rv2, veps2).then_inc(rv_ready, 1)
            dve.wait_ge(rs_ready, 1)
            do(tt(newton2, rstd2, rstd2, ALU.mult))
            do(tt(newton2, newton2, veps2, ALU.mult))
            do(ts(newton2, newton2, -0.5, 1.5, ALU.mult, ALU.add))
            do(tt(rstd2, rstd2, newton2, ALU.mult))
            for t in range(NT):
                ts(y_all[:, t, :], x1_all[:, t, :], mv2[:, t, 0:1], rstd2[:, t:t + 1], ALU.subtract, ALU.mult).then_inc(y_ready, 1)
            for g in range(0, 8, 2):
                dve.wait_ge(yT_done, g + 1)
                nc.vector.tensor_copy(yT[g // 4][:, (g % 4) * BANK:(g % 4) * BANK + BANK], ht_ps[:, 0:BANK]).then_inc(yT_dve, 1)
            dve.wait_ge(lg_done, 1)
            dve.wait_ge(const_ready, 1)
            dve.wait_ge(wg_in, 32)

            def wide(v):
                return v.unsqueeze(2).to_broadcast([P, NT, E])

            def over_tiles(v):
                return v.unsqueeze(1).to_broadcast([P, NT, E])

            def largest(values, top, low, pick):
                do(red(out=top, in_=values, axis=AX.X, op=ALU.max))
                do(tt(equal, values, wide(top), ALU.is_equal))
                do(nc.vector.scalar_tensor_tensor(out=cand, in0=equal, scalar=-2.0 * E, in1=iota_e, op0=ALU.mult, op1=ALU.add))
                do(red(out=low, in_=cand, axis=AX.X, op=ALU.min))
                do(tt(pick, cand, wide(low), ALU.is_equal))

            do(tt(logits, lg_ps[:, 0:NT * E].rearrange("p (t e) -> p t e", e=E), over_tiles(bg_bc[:, :]), ALU.add))
            largest(logits, max1, min1, pick1)
            do(nc.vector.scalar_tensor_tensor(out=rest, in0=pick1, scalar=LOW, in1=logits, op0=ALU.mult, op1=ALU.add))
            largest(rest, max2, min1, pick2)
            tt(picks[:, :, :], pick1, pick2, ALU.add).then_inc(picked, 1)
            tt(diff, max2, max1, ALU.subtract).then_inc(diff_ready, 1)
            dve.wait_ge(ediff_ready, 1)
            do(ts(wt1, ediff, 1.0, None, ALU.add))
            do(nc.vector.reciprocal(wt1, wt1))
            do(tt(wt2, ediff, wt1, ALU.mult))
            do(nc.vector.memset(cum[:, 0, :], 0.0))
            dve.wait_ge(ranked, 1)
            for t in range(NT):
                do(tt(cum[:, t + 1, :], cum[:, t, :], y_ps[1][:, t * E:t * E + E], ALU.add))
            do(tt(tmp, cum[:, NT, :].unsqueeze(2).to_broadcast([P, E, NT]), iota_j, ALU.is_gt))
            do(red(out=tiles_e, in_=tmp, axis=AX.X, op=ALU.add))
            do(ts(tiles_e, tiles_e, 1.0, None, ALU.max))
            do(tt(tmp, tri, tiles_e.unsqueeze(1).to_broadcast([P, E, E]), ALU.mult))
            do(red(out=end_e, in_=tmp, axis=AX.X, op=ALU.add))
            do(tt(base_e, end_e, tiles_e, ALU.subtract))
            do(ts(base_e, base_e, float(P), None, ALU.mult))
            do(tt(pos, y_ps[0][:, 0:NT * E].rearrange("p (t e) -> p t e", e=E), cum[:, 0:NT, :], ALU.add))
            do(tt(pos, pos, over_tiles(base_e), ALU.add))
            for k, pick in enumerate((pick1, pick2)):
                do(tt(tmp, pos, pick, ALU.mult))
                do(red(out=slot_fp[:, k, :], in_=tmp, axis=AX.X, op=ALU.add))
            nc.vector.tensor_copy(slot_of[:, :, :], slot_fp[:, :, :]).then_inc(slots_ready, 1)
            do(tt(ended[:, :, :], end_e[0:1].unsqueeze(1).to_broadcast([1, TILES, E]), tile_iota[:, :, :], ALU.is_le))
            do(red(out=tile_expert[:, :], in_=ended[:, :, :], axis=AX.X, op=ALU.add))
            do(nc.vector.tensor_copy(tile_end_i[:, :], end_e[0:1]))
            do(tt(over_pairs[:, :], tile_iota[:, 0:TILES:2, 0], end_e[0:1, E - 1:E].to_broadcast([1, TILES // 2]), ALU.is_lt))
            do(red(out=n_pairs[:, :], in_=over_pairs[:, :], axis=AX.X, op=ALU.add))
            do(ts(n_pairs_i[:, :], n_pairs[:, :], float(FEWEST), None, ALU.subtract))
            ts(tile_expert_i[:, :], tile_expert[:, :], float(E - 1), None, ALU.min).then_inc(table_ready, 1)

            def x_low(t, i):
                dve.wait_ge(x_hi, t + 1)
                wait(dve, h_done, t - 1)
                tt(xT_lo[:, i, :], xt_ps[:, 0:DC * P], xT_hi[:, i, :].bitcast(F32), ALU.subtract).then_inc(x_lo, 1)

            def pair(phase, j):
                for i in range(2):
                    s = 2 * j + i
                    if has(phase, i, 0):
                        e = expert_of(dve, s)
                        dve.wait_ge(h_done, s + 1)
                        wait(dve, ht_done, s - 1)
                        tt(hid[:, i, :], h_ps[:, :], b1_bc[:, bass.ds((e % 2) * HID, HID)], ALU.add).then_inc(h_biased, 1)
                    if has(phase, i, -1):
                        x_low(s + 1, 1 - i)
                    if has(phase, i, 1):
                        dve.wait_ge(h_hi, s)
                        wait(dve, y_done, s - 2)
                        tt(hT_lo[:, 1 - i, :], ht_ps[:, :], hT_hi[:, 1 - i, :].bitcast(F32), ALU.subtract).then_inc(h_lo, 1)
                    if has(phase, i, 2):
                        e = expert_of(dve, s - 2)
                        dve.wait_ge(y_done, s - 1)
                        wait(dve, sy_out[i], 16 * (j - 1))
                        tt(y_sb[:, i, :], y_ps[i][:, 0:D], b2_bc[:, bass.ds((e % 2) * D, D)], ALU.add).then_inc(y_biased, 1)

            x_low(0, 0)
            steps(dve, pair)
            for t in range(NT):
                dve.wait_ge(gathered[t], 16 * TOPK)
                nc.vector.scalar_tensor_tensor(out=part[t % 2], in0=got[0][t], scalar=wt1[:, t:t + 1], in1=x1_all[:, t, :],
                                               op0=ALU.mult, op1=ALU.add).then_inc(part_ready, 1)
                dve.wait_ge(part_ready, t + 1)
                if t >= 2:
                    dve.wait_ge(stored[t % 2], 16 * (t // 2))
                nc.vector.scalar_tensor_tensor(out=res[t % 2], in0=got[1][t], scalar=wt2[:, t:t + 1], in1=part[t % 2],
                                               op0=ALU.mult, op1=ALU.add).then_inc(res_ready, 1)

        @block.tensor
        def _(pe):
            pe.wait_ge(const_ready, 1)
            for g in range(8):
                k, q = g // 4, g % 4
                pe.wait_ge(y_ready, 4 * q + 4)
                if g >= 2:
                    pe.wait_ge(yT_dve if g % 2 == 0 else yT_act, g // 2)
                for i in range(4):
                    last = nc.tensor.transpose(ht_ps[:, (g % 2) * BANK + i * P:(g % 2) * BANK + i * P + P],
                                               y_all[:, 4 * q + i, k * P:k * P + P], ident2[:, :])
                last.then_inc(yT_done, 1)
            pe.wait_ge(wg_in, 32)
            pe.wait_ge(yT_dve, 4)
            pe.wait_ge(yT_act, 4)
            for t in range(NT):
                for k in range(DC):
                    last = nc.tensor.matmul(lg_ps[:, t * E:t * E + E], yT[k][:, t * P:t * P + P], wg_sb[:, k, :],
                                            start=k == 0, stop=k == DC - 1)
            last.then_inc(lg_done, 1)
            pe.wait_ge(picked, 1)
            flat = picks[:, :, :].rearrange("p t e -> p (t e)")
            nc.tensor.matmul(y_ps[0][:, 0:NT * E], before[:, :], flat, start=True, stop=True)
            nc.tensor.matmul(y_ps[1][:, 0:NT * E], ones[:, :], flat, start=True, stop=True).then_inc(ranked, 1)
            pe.wait_ge(table_ready, 1)

            def transpose_rows(t, i, j):
                pe.wait_ge(sx_in[i], 16 * j + 16)
                wait(pe, x_lo, t)
                for k in range(DC):
                    last = nc.tensor.transpose(xt_ps[:, k * P:k * P + P], x_in_sb[:, i, k * P:k * P + P], ident2[:, :])
                last.then_inc(xt_done, 1)

            def up(t, i):
                e = expert_of(pe, t)
                base = (e % 2) * WC
                pe.wait_ge(w1_ready, e + 1)
                wait(pe, h_biased, t)
                pe.wait_ge(x_lo, t + 1)
                for half in range(HID // BANK):
                    terms = [(x, w, k) for k in range(DC) for x, w in ((xT_hi, w_hi), (xT_hi, w_lo), (xT_lo, w_hi))]
                    for n_, (x, w, k) in enumerate(terms):
                        last = nc.tensor.matmul(h_ps[:, half * BANK:half * BANK + BANK], x[:, i, k * P:k * P + P],
                                                w[:, bass.ds(base + k * HID + half * BANK, BANK)],
                                                start=n_ == 0, stop=n_ == len(terms) - 1)
                last.then_inc(h_done, 1)

            def transpose_hidden(t, i):
                pe.wait_ge(gelu_done, t + 1)
                wait(pe, h_lo, t)
                for c in range(HC):
                    last = nc.tensor.transpose(ht_ps[:, c * P:c * P + P], hid[:, i, c:HID:HC], ident2[:, :])
                last.then_inc(ht_done, 1)

            def down(t, i):
                e = expert_of(pe, t)
                base = (e % 2) * WC + W1C
                pe.wait_ge(w2_ready, e + 1)
                pe.wait_ge(h_lo, t + 1)
                wait(pe, y_biased, t - 1)
                for c in range(HC):
                    for n_, (x, w) in enumerate(((hT_hi, w_hi), (hT_hi, w_lo), (hT_lo, w_hi))):
                        last = nc.tensor.matmul(y_ps[i][:, 0:D], x[:, i, c * P:c * P + P], w[:, bass.ds(base + c * D, D)],
                                                start=c == 0 and n_ == 0, stop=c == HC - 1 and n_ == 2)
                last.then_inc(y_done, 1)

            def pair(phase, j):
                for i in range(2):
                    s = 2 * j + i
                    if has(phase, i, 0):
                        up(s, i)
                    if has(phase, i, -1):
                        transpose_rows(s + 1, 1 - i, j + i)
                    if has(phase, i, 1):
                        transpose_hidden(s - 1, 1 - i)
                    if has(phase, i, 2):
                        down(s - 2, i)

            transpose_rows(0, 0, 0)
            steps(pe, pair)


def layer(nc, x, adj, x2, v, wg, bg, w1, b1, w2, b2, out):
    P = 128
    N, D = x.shape
    E = w1.shape[0]
    tiles = -(-(N * 2 // P + E - 1) // (N // P)) * (N // P)
    x1 = nc.dram_tensor("x1", [N, D], F32).ap()
    slots_x = nc.dram_tensor("slots_x", [tiles * P, D], F32).ap()
    slots_y = nc.dram_tensor("slots_y", [tiles * P, D], F32).ap()
    graph_attention(nc, x, adj, x2, v, x1, [slots_x, slots_y])
    expert_ffn(nc, x1, wg, bg, w1, b1, w2, b2, out, slots_x, slots_y)


_INS = ["x", "adj", "L0_gnn_x2", "L0_gnn_v", "L0_ffn_Wg", "L0_ffn_bg", "L0_ffn_W1", "L0_ffn_b1", "L0_ffn_W2", "L0_ffn_b2"]


def kernel(**inputs):
    import numpy as _np
    import concourse.bacc as _bacc
    from concourse import mybir as _mybir
    from concourse.bass_utils import run_bass_kernel_spmd as _run

    nc = _bacc.Bacc("TRN2", target_bir_lowering=False, num_devices=1)
    arrays, args = {}, []
    for name in _INS:
        a = _np.ascontiguousarray(inputs[name])
        arrays[f"in_{name}"] = a
        args.append(nc.dram_tensor(f"in_{name}", a.shape, _mybir.dt.from_np(a.dtype), kind="ExternalInput").ap())
    out = nc.dram_tensor("out", inputs["x"].shape, _mybir.dt.float32, kind="ExternalOutput").ap()
    layer(nc, *args, out)
    return _run(nc, [arrays], core_ids=[0]).results[0]["out"]
```

```python
from contextlib import ExitStack
import concourse.bass as bass
from concourse import mybir
F32, F32R, BF16, I32, U32 = mybir.dt.float32, mybir.dt.float32r, mybir.dt.bfloat16, mybir.dt.int32, mybir.dt.uint32
ALU = mybir.AluOpType
ACT = mybir.ActivationFunctionType
AX = mybir.AxisListType


def attend_and_route(nc, x, adj, x2, v, wg, bg, x1, slots_x, to_zero, routing):
    pick12, pos_all, diff_all, ahead, scattered = routing
    E = wg.shape[1]
    TOPK = 2
    N, D = x.shape
    H = 8
    DH = D // H
    P = 128
    NT = N // P
    KS = 3 * DH
    HALF = N // 2
    BANK = 512
    GRP = N // BANK
    BPG = BANK // P
    BATCH = 4
    SM = 4
    SCALE = DH ** -0.5
    MASKED = 9000000000000000.0
    EPS = 1e-5

    x_t = x.rearrange("(t p) d -> t p d", p=P)
    x_p = x.rearrange("(t p) d -> p t d", p=P)
    x2_p = x2.rearrange("(t p) d -> p t d", p=P)
    v_p = v.rearrange("(t p) d -> p t d", p=P)
    adj_t = adj.rearrange("(t p) m -> t p m", p=P)
    x1_t = x1.rearrange("(t p) d -> t p d", p=P)
    wg_p = wg.rearrange("(k p) e -> p k e", p=P)
    DC = D // P
    REGION = N + P
    zero_parts = to_zero.rearrange("(i c p) d -> i c p d", i=NT, p=P)

    ctx = ExitStack()
    with ctx:
        def sb(name, shape, dt):
            return ctx.enter_context(nc.sbuf_tensor(name, shape, dt))

        def sem(name):
            return ctx.enter_context(nc.semaphore(name))

        keysT = sb("keysT", [KS, H, N], F32R)
        scores = sb("scores", [P, SM, N], F32)
        probsT = sb("probsT", [P, H, NT, P], F32)
        values = sb("values", [P, NT, D], F32)
        adj_bf = sb("adj_bf", [P, N], BF16)
        mask = sb("mask", [P, N], BF16)
        queriesT = sb("queriesT", [KS, H, P], F32R)
        q_nat = sb("q_nat", [P, H, 3, DH], F32R)
        x_q = sb("x_q", [P, D], F32)
        x_mid = sb("x_mid", [P, D], F32)
        xn = sb("xn", [P, D], F32)
        x_res = sb("x_res", [P, D], F32)
        att = sb("att", [P, D], F32)
        x1_sb = sb("x1_sb", [P, D], F32)
        outT = sb("outT", [P, 2, P], F32)
        ident = sb("ident", [P, P], F32)
        zeros = sb("zeros", [P, D], F32)
        row_min = sb("row_min", [P, 2, 4], F32)
        row_sum = sb("row_sum", [P, NT * H], F32)
        r_den = sb("r_den", [P, H], F32)
        mean_var = sb("mean_var", [P, NT, 2], F32)
        nscale = sb("nscale", [P, NT], F32)
        stats = x1_sb[:, 0:6 * NT].rearrange("p (t c) -> p t c", c=6)
        veps, rv, rstd, newton = (x1_sb[:, (6 + i) * NT:(7 + i) * NT] for i in range(4))
        wg_sb = sb("wg_sb", [P, DC, E], F32)
        bg_bc = sb("bg_bc", [P, E], F32)
        before = sb("before", [P, P], BF16)
        ones = sb("ones", [P, P], BF16)
        iota_e = sb("iota_e", [P, E], F32)
        y_mid = sb("y_mid", [P, D], F32)
        y_row = sb("y_row", [P, D], F32)
        yT = sb("yT", [P, DC * P], F32)
        y_stats = sb("y_stats", [P, 6], F32)
        y_mv = sb("y_mv", [P, 2], F32)
        y_small = sb("y_small", [P, 8], F32)
        y_veps, y_rstd, y_newton = (y_small[:, i:i + 1] for i in range(3))
        y_bits = sb("y_bits", [P, 1], I32)
        lg = sb("lg", [P, E], F32)
        top8 = sb("top8", [P, 8], F32)
        top8_at = sb("top8_at", [P, 8], U32)
        top_at = sb("top_at", [P, TOPK], F32)
        pos = xn[:, TOPK * E:TOPK * E + E]
        at12 = xn[:, 0:TOPK * E].rearrange("p (k e) -> p k e", e=E)
        pick = sb("pick", [P, TOPK, E], F32)
        picks = sb("picks", [P, E], BF16)
        ranks = sb("ranks", [P, 2 * E], F32)
        slot_of = sb("slot_of", [P, TOPK], U32)
        x_all = probsT[:, 0:2, :, :].rearrange("p a t n -> p (a t n)").rearrange("p (t d) -> p t d", d=D)
        x2_all = scores[:, 0:2, :].rearrange("p a n -> p (a n)").rearrange("p (t d) -> p t d", d=D)
        k_nat = [scores[:, 2 + i // 2, i % 2 * HALF:i % 2 * HALF + H * KS].rearrange("p (h c d) -> p h c d", c=3, d=DH)
                 .bitcast(F32R) for i in range(4)]

        s_ps = [ctx.enter_context(nc.psum_tensor(f"s_ps{i}", [P, HALF], F32)) for i in range(2)]
        t_ps = [ctx.enter_context(nc.psum_tensor(f"t_ps{i}", [P, BANK], F32)) for i in range(2)]
        o_ps = ctx.enter_context(nc.psum_tensor("o_ps", [P, BANK], F32))
        a_ps = ctx.enter_context(nc.psum_tensor("a_ps", [P, BANK], F32))

        x_in, v_in, zeros_ready, zeroed = sem("x_in"), sem("v_in"), sem("zeros_ready"), sem("zeroed")
        x2_in = [sem(f"x2_in{i}") for i in range(4)]
        ident_zero, ident_ready = sem("ident_zero"), sem("ident_ready")
        k_hi, k_split, k_tr, k_dve, k_act = sem("k_hi"), sem("k_split"), sem("k_tr"), sem("k_dve"), sem("k_act")
        ln_step, rv_ready, rs_ready, ln_ready = sem("ln_step"), sem("rv_ready"), sem("rs_ready"), sem("ln_ready")
        adj_in, xq_in, xr_in, x1_out = sem("adj_in"), sem("xq_in"), sem("xr_in"), sem("x1_out")
        mask_done, dve_waited = sem("mask_done"), sem("dve_waited")
        xn_done, hi_done, q_split = sem("xn_done"), sem("hi_done"), sem("q_split")
        q_tr, q_ev = sem("q_tr"), sem("q_ev")
        s_done, first_min, row_ready, exp_done = sem("s_done"), sem("first_min"), sem("row_ready"), sem("exp_done")
        t_done, dve_ev, act_ev = sem("t_done"), sem("dve_ev"), sem("act_ev")
        pv_done, outT_ev, o_tr = sem("pv_done"), sem("outT_ev"), sem("o_tr")
        den_ready, att_ready, x1_ready = sem("den_ready"), sem("att_ready"), sem("x1_ready")

        wg_in, stats_step, stats_ready = sem("wg_in"), sem("stats_step"), sem("stats_ready")
        route_step, pool_waited, row_normed = sem("route_step"), sem("pool_waited"), sem("row_normed")
        yT_done, yT_ev, lg_done, lg_ready = sem("yT_done"), sem("yT_ev"), sem("lg_done"), sem("lg_ready")
        picked, ranked, ranks_ready, slots_found = sem("picked"), sem("ranked"), sem("ranks_ready"), sem("slots_found")
        lg_step, centred = sem("lg_step"), sem("centred")
        consts_ready = sem("consts_ready")

        DVE_GROUPS = [(0,), (0, 2)]
        ACT_GROUPS = [(1, 2, 3), (1, 3)]

        def copied(groups, it, h, g=GRP - 1):
            per = sum(len(groups[i % 2]) for i in range(H))
            return it * per + sum(len(groups[i % 2]) for i in range(h)) + sum(1 for i in groups[h % 2] if i <= g)

        FIRST, MID, LAST, DRAIN = range(4)

        def back(phase, it, h, d):
            if phase == FIRST and h < d or phase == DRAIN and h >= d:
                return None
            return (it, h - d) if h >= d else (it - 1, h - d + H)

        def wait(eng, s, value):
            if not isinstance(value, int) or value > 0:
                eng.wait_ge(s, value)

        def tiles(eng, step):
            step(FIRST, 0)
            step(MID, 1)
            step(MID, 2)
            with eng.Fori(3, NT - 1) as it:
                step(MID, it)
            step(LAST, NT - 1)
            step(DRAIN, NT)

        def to_route(it):
            return None if isinstance(it, int) and it < 2 else it - 2

        ACT_KEYS = (3, 7, 8, 9, 11, 15)

        def keys_of(q):
            return range(4 * q, 4 * q + 4)

        def keys_copied(eng, t):
            if t >= 0:
                by_act = sum(1 for i in ACT_KEYS if i <= t)
                if t in ACT_KEYS:
                    eng.wait_ge(k_act, by_act)
                else:
                    eng.wait_ge(k_dve, t + 1 - by_act)

        block = ctx.enter_context(nc.Block())

        @block.sync
        def _(sp):
            for i in range(4):
                if i == 2:
                    sp.dma_start(x_all, x_p).then_inc(x_in, 16)
                sp.dma_start(x2_all[:, 4 * i:4 * i + 4, :], x2_p[:, 4 * i:4 * i + 4, :]).then_inc(x2_in[i], 16)
            sp.dma_start(x_q[:, :], x_t[0]).then_inc(xq_in, 16)
            sp.dma_start(values[:, :, :], v_p).then_inc(v_in, 16)

            sp.dma_start(wg_sb[:, :, :], wg_p).then_inc(wg_in, 16)
            sp.dma_start(bg_bc[:, :], bg.rearrange("(a e) -> a e", a=1).to_broadcast([P, E])).then_inc(wg_in, 16)
            sp.wait_ge(zeros_ready, 1)

            def tile(phase, it):
                if phase in (FIRST, MID):
                    wait(sp, xn_done, it + 1)
                    sp.dma_start(x_q[:, :], x_t[it + 1]).then_inc(xq_in, 16)
                if phase != DRAIN:
                    sp.dma_start(zero_parts[bass.ds(it, 1)].rearrange("a c p d -> p (a c) d"),
                                 zeros[:, :].unsqueeze(1).to_broadcast([P, zero_parts.shape[1], D])).then_inc(zeroed, 16)
                if phase != FIRST:
                    wait(sp, x1_ready, it - 1)
                    sp.dma_start(x_res[:, :], x_t[it - 1]).then_inc(xr_in, 16)
                    wait(sp, x1_ready, it)
                    sp.dma_start(x1_t[it - 1], x1_sb[:, :]).then_inc(x1_out, 16)

            tiles(sp, tile)
            sp.wait_ge(x1_out, 16 * NT)
            sp.wait_ge(zeroed, 16 * NT)

        @block.gpsimd
        def _(pool):
            pool.dma_start(adj_bf[:, :], adj_t[0]).then_inc(adj_in, 16)
            nc.gpsimd.memset(ident[:, :], 0.0).then_inc(ident_zero, 1)
            nc.gpsimd.memset(zeros[:, :], 0.0).then_inc(zeros_ready, 1)
            pool.wait_ge(ident_zero, 1)
            nc.gpsimd.affine_select(out=ident[:, :], in_=ident[:, :], compare_op=ALU.not_equal, fill=1.0, base=0,
                                    pattern=[[-1, P]], channel_multiplier=1).then_inc(ident_ready, 1)

            for q in range(4):
                for t in keys_of(q):
                    pool.wait_ge(k_hi, 2 * t + 2)
                    nc.gpsimd.tensor_tensor(out=k_nat[t % 4][:, :, 1, :], in0=x2_all[:, t, :].rearrange("p (h d) -> p h d", d=DH),
                                            in1=k_nat[t % 4][:, :, 0, :].bitcast(F32), op=ALU.subtract).then_inc(k_split, 1)

            def split_queries(t):
                wait(pool, xq_in, 16 * t + 16)
                if isinstance(t, int) and t == 0:
                    pool.wait_ge(ln_ready, 1)
                wait(pool, q_split, t)
                row = [P, D]
                nc.gpsimd.tensor_tensor(out=x_mid[:, :], in0=x_q[:, :], in1=mean_var[:, bass.ds(t, 1), 0].to_broadcast(row),
                                        op=ALU.subtract).then_inc(xn_done, 1)
                wait(pool, xn_done, t + 1)
                wait(pool, q_tr, 2 * t)
                scale = nscale[:, bass.ds(t, 1)].to_broadcast(row)
                nc.gpsimd.tensor_tensor(out=xn[:, :], in0=x_mid[:, :], in1=scale, op=ALU.mult)
                for c in range(2):
                    nc.gpsimd.tensor_tensor(out=q_nat[:, :, c, :], in0=x_mid[:, :].rearrange("p (h d) -> p h d", d=DH),
                                            in1=nscale[:, bass.ds(t, 1)].unsqueeze(2).to_broadcast([P, H, DH]),
                                            op=ALU.mult).then_inc(hi_done, 1)
                wait(pool, hi_done, 2 * t + 2)
                nc.gpsimd.tensor_tensor(out=q_nat[:, :, 2, :], in0=xn[:, :].rearrange("p (h d) -> p h d", d=DH),
                                        in1=q_nat[:, :, 0, :].bitcast(F32), op=ALU.subtract).then_inc(q_split, 1)

            split_queries(0)
            nc.gpsimd.memset(ones[:, :], 1.0)
            nc.gpsimd.memset(before[:, :], 1.0).then_inc(route_step, 1)
            nc.gpsimd.iota(iota_e[:, :], pattern=[[1, E]], base=0, channel_multiplier=0, allow_small_or_imprecise_dtypes=True)
            nc.gpsimd.iota(ahead[:, :], pattern=[[REGION, E]], base=0, channel_multiplier=0,
                           allow_small_or_imprecise_dtypes=True).then_inc(route_step, 1)
            pool.wait_ge(route_step, 2)
            nc.gpsimd.affine_select(out=before[:, :], in_=before[:, :], compare_op=ALU.is_gt, fill=0.0, base=0,
                                    pattern=[[1, P]], channel_multiplier=-1).then_inc(consts_ready, 1)

            NORM, PICK, SLOT = 12, 2, 8
            tt, ts = nc.gpsimd.tensor_tensor, nc.gpsimd.tensor_scalar

            def chain(r, first):
                n = [2 + first]

                def do(ins):
                    n[0] += 1
                    ins.then_inc(route_step, 1)
                    pool.wait_ge(route_step, (NORM + PICK + SLOT) * r + n[0])
                    pool.sem_inc(pool_waited, 1)
                return do

            def normalise(r):
                do = chain(r, 0)
                pool.wait_ge(stats_ready, r + 1)
                pool.sem_inc(pool_waited, 1)
                for _ in range(3):
                    do(tt(y_newton, y_rstd, y_rstd, ALU.mult))
                    do(tt(y_newton, y_newton, y_veps, ALU.mult))
                    do(ts(y_newton, y_newton, -0.5, 1.5, ALU.mult, ALU.add))
                    do(tt(y_rstd, y_rstd, y_newton, ALU.mult))
                wait(pool, scattered, 16 * TOPK * r)
                pool.sem_inc(pool_waited, 1)
                tt(y_row[:, :], y_mid[:, :], y_rstd.to_broadcast([P, D]), ALU.mult).then_inc(row_normed, 1)

            def pick_experts(r):
                do = chain(r, NORM)
                pool.wait_ge(lg_ready, r + 1)
                if isinstance(r, int) and r == 0:
                    pool.wait_ge(consts_ready, 1)
                pool.sem_inc(pool_waited, 1)
                ts(pick[:, 0, :], iota_e[:, :], top_at[:, 0:1], None, ALU.is_equal)
                do(ts(pick[:, 1, :], iota_e[:, :], top_at[:, 1:2], None, ALU.is_equal))
                tt(picks[:, :], pick[:, 0, :], pick[:, 1, :], ALU.add).then_inc(picked, 1)
                nc.gpsimd.tensor_copy(pick12[:, :, bass.ds(r, 1), :].rearrange("p k a e -> p k (a e)"), pick[:, :, :])
                do(tt(diff_all[:, bass.ds(r, 1)], top8[:, 1:2], top8[:, 0:1], ALU.subtract))

            def scatter(r):
                do = chain(r, NORM + PICK)
                pool.wait_ge(ranks_ready, r + 1)
                pool.sem_inc(pool_waited, 1)
                tt(pos_all[:, bass.ds(r, 1), :].rearrange("p a e -> p (a e)"), ranks[:, 0:E], ahead[:, :], ALU.add)
                do(tt(pos, ranks[:, 0:E], ahead[:, :], ALU.add))
                do(tt(ahead[:, :], ahead[:, :], ranks[:, E:2 * E], ALU.add))
                do(tt(at12[:, :, :], pick[:, :, :], pos.unsqueeze(1).to_broadcast([P, TOPK, E]), ALU.mult))
                for half in (E // 2, E // 4, E // 8, E // 16):
                    do(tt(at12[:, :, 0:half], at12[:, :, 0:half], at12[:, :, half:2 * half], ALU.add))
                do(nc.gpsimd.tensor_copy(slot_of[:, :], at12[:, :, 0]))
                pool.sem_inc(slots_found, 1)
                for k in range(TOPK):
                    pool.indirect_dma_start(out=slots_x[:, :], out_offset=bass.IndirectOffsetOnAxis(ap=slot_of[:, k:k + 1], axis=0),
                                            in_=y_row[:, :], in_offset=None).then_inc(scattered, 16)

            def tile(phase, it):
                r = to_route(it)
                if phase in (FIRST, MID):
                    wait(pool, mask_done, 2 * it + 2)
                    pool.dma_start(adj_bf[:, :], adj_t[it + 1]).then_inc(adj_in, 16)
                if r is not None:
                    normalise(r)
                if phase in (FIRST, MID):
                    split_queries(it + 1)
                if r is not None:
                    pick_experts(r)
                if phase != FIRST:
                    wait(pool, xr_in, 16 * it)
                    wait(pool, att_ready, it)
                    wait(pool, x1_out, 16 * (it - 1))
                    nc.gpsimd.tensor_tensor(out=x1_sb[:, :], in0=att[:, :], in1=x_res[:, :], op=ALU.add).then_inc(x1_ready, 1)
                if r is not None:
                    scatter(r)

            tiles(pool, tile)
            normalise(NT - 1)
            pick_experts(NT - 1)
            scatter(NT - 1)

        @block.scalar
        def _(act):
            def key_high(t):
                wait(act, k_tr, t - 3)
                for c in (0, 2):
                    nc.scalar.copy(k_nat[t % 4][:, :, c, :], x2_all[:, t, :].rearrange("p (h d) -> p h d", d=DH)).then_inc(k_hi, 1)

            def copy_keys(t):
                act.wait_ge(k_tr, t + 1)
                nc.scalar.copy(keysT[:, :, t * P:t * P + P], s_ps[t % 2][0:KS, :].rearrange("p (h n) -> p h n", n=P)
                               ).then_inc(k_act, 1)

            for q in range(4):
                act.wait_ge(x2_in[q], 16)
                for t in keys_of(q):
                    key_high(t)
                    if t - 2 in ACT_KEYS:
                        copy_keys(t - 2)
                if q == 2:
                    act.wait_ge(rv_ready, 1)
                    nc.scalar.activation(rstd[:, :], rv[:, :], ACT.Sqrt).then_inc(rs_ready, 1)
            copy_keys(NT - 1)

            def copy_queries(t, half):
                wait(act, q_tr, 2 * t + half + 1)
                wait(act, s_done, 2 * (H * (t - 1) + BATCH * half + BATCH))
                nc.scalar.copy(queriesT[:, BATCH * half:BATCH * half + BATCH, :],
                               a_ps[0:KS, :].rearrange("p (h n) -> p h n", n=P)).then_inc(q_ev, 1)

            copy_queries(0, 0)

            def tile(phase, it):
                for h in range(H):
                    if phase in (FIRST, MID, LAST) and h == 1:
                        copy_queries(it, 1)
                    if h == 3 and to_route(it) is not None:
                        copy_rows(to_route(it))
                    two = back(phase, it, h, 2)
                    if two is not None:
                        copy_group(*two, 1)
                    prev = back(phase, it, h, 1)
                    if prev is not None:
                        t, g = prev
                        wait(act, row_ready, H * t + g + 1)
                        buf = scores[:, g % SM, :]
                        nc.scalar.activation(buf, buf, ACT.Exp, bias=row_min[:, 1, g % 4:g % 4 + 1], scale=-1.0,
                                             accum_out=row_sum[:, bass.ds(t * H + g, 1)]).then_inc(exp_done, 1)
                    if two is not None:
                        for grp in ACT_GROUPS[two[1] % 2][1:]:
                            copy_group(*two, grp)
                    if phase in (FIRST, MID) and h == 4:
                        copy_queries(it + 1, 0)

            def copy_rows(r):
                act.wait_ge(yT_done, r + 1)
                wait(act, lg_done, r)
                nc.scalar.copy(yT[:, :], a_ps[:, 0:DC * P]).then_inc(yT_ev, 1)

            def copy_group(t, g, grp):
                wait(act, t_done, GRP * (H * t + g) + grp + 1)
                if not (isinstance(t, int) and t == 0):
                    act.wait_ge(pv_done, 2 * t - 1 + g // BATCH)
                nc.scalar.copy(probsT[:, g, BPG * grp:BPG * grp + BPG, :],
                               t_ps[grp % 2][:, :].rearrange("p (c n) -> p c n", n=P)).then_inc(act_ev, 1)

            tiles(act, tile)
            copy_rows(NT - 1)

        @block.vector
        def _(dve):
            n_ln = [0]

            def ln(ins):
                n_ln[0] += 1
                ins.then_inc(ln_step, 1)
                dve.wait_ge(ln_step, n_ln[0])

            def copy_keys(q):
                for t in keys_of(q):
                    if t in ACT_KEYS:
                        continue
                    dve.wait_ge(k_tr, t + 1)
                    nc.vector.tensor_copy(out=keysT[:, :, t * P:t * P + P],
                                          in_=s_ps[t % 2][0:KS, :].rearrange("p (h n) -> p h n", n=P)).then_inc(k_dve, 1)

            copy_keys(0)
            copy_keys(1)
            dve.wait_ge(x_in, 16)
            for t in range(NT):
                last = nc.vector.bn_stats(out=stats[:, t, :], in_=x_all[:, t, :])
            ln(last)
            for t in range(NT):
                last = nc.vector.bn_aggr(out=mean_var[:, t, :], in_=stats[:, t, :])
            ln(last)
            ln(nc.vector.tensor_scalar(veps[:, :], mean_var[:, :, 1], EPS, None, ALU.add))
            ln(nc.vector.reciprocal(rv[:, :], veps[:, :]))
            nc.vector.tensor_scalar(rv[:, :], rv[:, :], 1.0, None, ALU.mult).then_inc(rv_ready, 1)
            copy_keys(2)
            dve.wait_ge(rs_ready, 1)
            ln(nc.vector.tensor_tensor(newton[:, :], rstd[:, :], rstd[:, :], ALU.mult))
            ln(nc.vector.tensor_tensor(newton[:, :], newton[:, :], veps[:, :], ALU.mult))
            ln(nc.vector.tensor_scalar(newton[:, :], newton[:, :], -0.5, 1.5, ALU.mult, ALU.add))
            ln(nc.vector.tensor_tensor(rstd[:, :], rstd[:, :], newton[:, :], ALU.mult))
            nc.vector.tensor_scalar(nscale[:, :], rstd[:, :], -SCALE, None, ALU.mult).then_inc(ln_ready, 1)
            copy_keys(3)

            def mask_half(t, half, read):
                if half == 0:
                    dve.wait_ge(adj_in, 16 * t + 16)
                wait(dve, read, H * t)
                cols = slice(half * HALF, half * HALF + HALF)
                nc.vector.tensor_scalar(mask[:, cols], adj_bf[:, cols], 0.0, MASKED, ALU.is_le, ALU.mult).then_inc(mask_done, 1)

            mask_half(0, 0, first_min)
            mask_half(0, 1, row_ready)

            def slot_free(eng, t, g):
                if not (isinstance(t, int) and t == 0):
                    eng.wait_ge(pv_done, 2 * t - 1 + g // BATCH)

            def find_stats(r, step):
                if step == 0:
                    dve.wait_ge(x1_ready, r + 1)
                    nc.vector.bn_stats(out=y_stats[:, :], in_=x1_sb[:, :]).then_inc(stats_step, 1)
                    return
                dve.wait_ge(stats_step, 4 * r + step if step < 3 else 4 * r + step - 1)
                if step == 1:
                    wait(dve, row_normed, r)
                    dve.sem_inc(dve_waited, 1)
                    nc.vector.bn_aggr(out=y_mv[:, :], in_=y_stats[:, :]).then_inc(stats_step, 1)
                elif step == 2:
                    wait(dve, yT_done, r)
                    dve.sem_inc(dve_waited, 1)
                    nc.vector.tensor_scalar(y_mid[:, :], x1_sb[:, :], y_mv[:, 0:1], None, ALU.subtract).then_inc(centred, 1)
                    nc.vector.tensor_scalar(y_veps, y_mv[:, 1:2], EPS, None, ALU.add).then_inc(stats_step, 1)
                elif step == 4:
                    dve.sem_inc(dve_waited, 1)
                    nc.vector.tensor_scalar(y_bits[:, :], y_veps.bitcast(I32), 1, None, ALU.logical_shift_right).then_inc(stats_step, 1)
                elif step == 5:
                    dve.sem_inc(dve_waited, 1)
                    nc.vector.tensor_scalar(y_rstd.bitcast(I32), y_bits[:, :], -1.0, float(0x5f3759df), ALU.mult, ALU.add
                                            ).then_inc(stats_ready, 1)

            def find_experts(r, step):
                if step == 0:
                    dve.wait_ge(lg_done, r + 1)
                    wait(dve, picked, r)
                    if isinstance(r, int) and r == 0:
                        dve.wait_ge(wg_in, 32)
                    dve.wait_ge(row_normed, r + 1)
                    dve.sem_inc(dve_waited, 1)
                    nc.vector.scalar_tensor_tensor(out=lg[:, :], in0=a_ps[:, DC * P:DC * P + E], scalar=y_rstd, in1=bg_bc[:, :],
                                                   op0=ALU.mult, op1=ALU.add).then_inc(lg_step, 1)
                    return
                dve.wait_ge(lg_step, 3 * r + step)
                dve.sem_inc(dve_waited, 1)
                if step == 1:
                    nc.vector.max(out=top8[:, :], in_=lg[:, :]).then_inc(lg_step, 1)
                elif step == 2:
                    nc.vector.max_index(out=top8_at[:, :], in_max=top8[:, :], in_values=lg[:, :]).then_inc(lg_step, 1)
                else:
                    nc.vector.tensor_copy(top_at[:, :], top8_at[:, 0:TOPK]).then_inc(lg_ready, 1)

            def route_step_at(it, h, half):
                r = to_route(it)
                if r is None:
                    return
                if h < 3 and 2 * h + half in (0, 1, 2, 4, 5):
                    find_stats(r, 2 * h + half)
                if h in (4, 5):
                    find_experts(r, 2 * (h - 4) + half)

            def copy_ranks(r):
                dve.wait_ge(ranked, r + 1)
                wait(dve, slots_found, r)
                nc.vector.tensor_copy(ranks[:, :], a_ps[:, DC * P:DC * P + 2 * E]).then_inc(ranks_ready, 1)

            def tile(phase, it):
                for h in range(H):
                    u = H * it + h
                    if phase != DRAIN:
                        dve.wait_ge(s_done, 2 * u + 1)
                        dve.wait_ge(mask_done, 2 * it + 1)
                        if back(phase, it, h, SM) is not None:
                            dve.wait_ge(t_done, GRP * (u - SM) + GRP)
                        dve.sem_inc(dve_waited, 1)
                        nc.vector.tensor_tensor_reduce(
                            out=scores[:, h % SM, 0:HALF], in0=s_ps[0][:, :], in1=mask[:, 0:HALF], scale=1.0, scalar=3e38,
                            op0=ALU.add, op1=ALU.min, accum_out=row_min[:, 0, h % 4:h % 4 + 1]).then_inc(first_min, 1)
                    if phase in (FIRST, MID) and h == H - 1:
                        mask_half(it + 1, 0, first_min)
                    prev = back(phase, it, h, 2)
                    if prev is not None:
                        t, g = prev
                        slot_free(dve, t, g)
                        for grp in DVE_GROUPS[g % 2]:
                            if grp:
                                continue
                            dve.wait_ge(t_done, GRP * (H * t + g) + grp + 1)
                            nc.vector.tensor_copy(out=probsT[:, g, BPG * grp:BPG * grp + BPG, :],
                                                  in_=t_ps[grp % 2][:, :].rearrange("p (c n) -> p c n", n=P)).then_inc(dve_ev, 1)
                    if phase != FIRST and h == 7:
                        dve.wait_ge(exp_done, H * it)
                        wait(dve, att_ready, it - 1)
                        nc.vector.reciprocal(r_den[:, :], row_sum[:, bass.ds((it - 1) * H, H)]).then_inc(den_ready, 1)
                        dve.wait_ge(den_ready, it)
                        dve.wait_ge(o_tr, it)
                        wait(dve, x1_ready, it - 1)
                        nc.vector.tensor_tensor(att[:, :].rearrange("p (h d) -> p h d", d=DH),
                                                a_ps[:, 0:D].rearrange("p (h d) -> p h d", d=DH),
                                                r_den[:, :].unsqueeze(2).to_broadcast([P, H, DH]), ALU.mult).then_inc(att_ready, 1)
                        if to_route(it) is not None:
                            copy_ranks(to_route(it))
                    route_step_at(it, h, 0)
                    if phase != DRAIN:
                        dve.wait_ge(s_done, 2 * u + 2)
                        dve.wait_ge(mask_done, 2 * it + 2)
                        dve.wait_ge(first_min, u + 1)
                        dve.sem_inc(dve_waited, 1)
                        dve.sem_inc(dve_waited, 1)
                        nc.vector.tensor_tensor_reduce(
                            out=scores[:, h % SM, HALF:N], in0=s_ps[1][:, :], in1=mask[:, HALF:N], scale=1.0,
                            scalar=row_min[:, 0, h % 4:h % 4 + 1], op0=ALU.add, op1=ALU.min,
                            accum_out=row_min[:, 1, h % 4:h % 4 + 1]).then_inc(row_ready, 1)
                    if phase in (FIRST, MID) and h == H - 1:
                        mask_half(it + 1, 1, row_ready)
                    route_step_at(it, h, 1)
                    if prev is not None:
                        for grp in DVE_GROUPS[g % 2]:
                            if not grp:
                                continue
                            dve.wait_ge(t_done, GRP * (H * t + g) + grp + 1)
                            nc.vector.tensor_copy(out=probsT[:, g, BPG * grp:BPG * grp + BPG, :],
                                                  in_=t_ps[grp % 2][:, :].rearrange("p (c n) -> p c n", n=P)).then_inc(dve_ev, 1)
                    if phase != FIRST and h in (1, 5):
                        b = 2 * it - 2 + h // BATCH
                        dve.wait_ge(pv_done, b + 1)
                        wait(dve, o_tr, it - 1)
                        nc.vector.tensor_copy(out=outT[:, h // BATCH, :], in_=o_ps[:, 0:P]).then_inc(outT_ev, 1)

            tiles(dve, tile)
            for i in (0, 1, 2, 4, 5):
                find_stats(NT - 1, i)
            for i in range(4):
                find_experts(NT - 1, i)
            copy_ranks(NT - 1)

        @block.tensor
        def _(pe):
            pe.wait_ge(ident_ready, 1)

            for q in range(4):
                for t in keys_of(q):
                    pe.wait_ge(k_split, t + 1)
                    pe.wait_ge(k_hi, 2 * t + 2)
                    keys_copied(pe, t - 2)
                    for h in range(H):
                        last = nc.tensor.transpose(s_ps[t % 2][0:KS, h * P:h * P + P],
                                                   k_nat[t % 4][:, h, :, :].bitcast(F32).rearrange("p c d -> p (c d)"), ident[:, :])
                    last.then_inc(k_tr, 1)

            def transpose_queries(t, half):
                pe.wait_ge(q_split, t + 1)
                pe.wait_ge(hi_done, 2 * t + 2)
                if half == 0:
                    wait(pe, q_ev, 2 * t)
                    if to_route(t - 1) is not None:
                        pe.wait_ge(lg_step, 3 * (t - 3) + 1)
                else:
                    wait(pe, att_ready, t - 1)
                    if to_route(t - 1) is not None:
                        pe.wait_ge(ranks_ready, t - 2)
                    pe.wait_ge(q_ev, 2 * t + 1)
                for i in range(BATCH):
                    last = nc.tensor.transpose(a_ps[0:KS, i * P:i * P + P],
                                               q_nat[:, BATCH * half + i, :, :].bitcast(F32).rearrange("p c d -> p (c d)"),
                                               ident[:, :])
                last.then_inc(q_tr, 1)

            def score(t, h, half):
                u = H * t + h
                if half == 0:
                    pe.wait_ge(q_ev, 2 * t + 1 + h // BATCH)
                    wait(pe, first_min, u)
                    if isinstance(t, int) and t == 0:
                        keys_copied(pe, NT - 2)
                        keys_copied(pe, NT - 1)
                else:
                    wait(pe, row_ready, u)
                for c in range(HALF // BANK):
                    m = half * HALF + c * BANK
                    last = nc.tensor.matmul(s_ps[half][:, c * BANK:c * BANK + BANK], queriesT[:, h, :], keysT[:, h, m:m + BANK],
                                            start=True, stop=True)
                last.then_inc(s_done, 1)

            def transpose_probs(t, h, grp):
                u = H * t + h
                if grp == 0:
                    pe.wait_ge(exp_done, u + 1)
                before = (t, h, grp - 2) if grp >= 2 else (t, h - 1, grp + 2) if h else (t - 1, H - 1, grp + 2)
                tt, hh, gg = before
                if gg in DVE_GROUPS[hh % 2]:
                    wait(pe, dve_ev, copied(DVE_GROUPS, tt, hh, gg))
                else:
                    wait(pe, act_ev, copied(ACT_GROUPS, tt, hh, gg))
                for i in range(BPG):
                    m = (grp * BPG + i) * P
                    last = nc.tensor.transpose(t_ps[grp % 2][:, i * P:i * P + P], scores[:, h % SM, m:m + P], ident[:, :])
                last.then_inc(t_done, 1)

            def value_products(t, half, eighth):
                if eighth == 0:
                    hh = BATCH * half + BATCH - 1
                    pe.wait_ge(dve_ev, copied(DVE_GROUPS, t, hh))
                    pe.wait_ge(act_ev, copied(ACT_GROUPS, t, hh))
                    wait(pe, outT_ev, 2 * t + half)
                    if isinstance(t, int) and t == 0:
                        pe.wait_ge(v_in, 16)
                for c in range(eighth * NT // 8, (eighth + 1) * NT // 8):
                    for i in range(BATCH):
                        h = BATCH * half + i
                        last = nc.tensor.matmul(o_ps[DH * i:DH * i + DH, 0:P], values[:, c, h * DH:h * DH + DH],
                                                probsT[:, h, c, :], start=c == 0, stop=c == NT - 1,
                                                tile_position=(0, DH * i))
                if eighth == 7:
                    last.then_inc(pv_done, 1)

            def transpose_rows(r, queries):
                pe.wait_ge(centred, r + 1)
                pe.wait_ge(q_ev, queries)
                pe.wait_ge(att_ready, r + 1)
                wait(pe, ranks_ready, r)
                for k in range(DC):
                    last = nc.tensor.transpose(a_ps[:, k * P:k * P + P], y_mid[:, k * P:k * P + P], ident[:, :])
                last.then_inc(yT_done, 1)

            def find_logits(r):
                pe.wait_ge(yT_ev, r + 1)
                if isinstance(r, int) and r == 0:
                    pe.wait_ge(wg_in, 32)
                for k in range(DC):
                    last = nc.tensor.matmul(a_ps[:, DC * P:DC * P + E], yT[:, k * P:k * P + P], wg_sb[:, k, :],
                                            start=k == 0, stop=k == DC - 1)
                last.then_inc(lg_done, 1)

            def rank(r):
                pe.wait_ge(picked, r + 1)
                pe.wait_ge(lg_step, 3 * r + 1)
                nc.tensor.matmul(a_ps[:, DC * P:DC * P + E], before[:, :], picks[:, :], start=True, stop=True)
                nc.tensor.matmul(a_ps[:, DC * P + E:DC * P + 2 * E], ones[:, :], picks[:, :], start=True, stop=True).then_inc(ranked, 1)

            def transpose_out(phase, t):
                pe.wait_ge(outT_ev, 2 * t + 2)
                pe.wait_ge(q_ev, 2 * NT if phase in (LAST, DRAIN) else 2 * t + 5)
                if to_route(t + 1) is not None:
                    rank(to_route(t + 1))
                for half in range(2):
                    last = nc.tensor.transpose(a_ps[:, half * P:half * P + P], outT[:, half, :], ident[:, :])
                last.then_inc(o_tr, 1)

            transpose_queries(0, 0)
            score(0, 0, 0)
            score(0, 0, 1)

            def tile(phase, it):
                for h in range(H):
                    ahead = phase in (FIRST, MID) or phase == LAST and h < H - 1
                    nxt = (it, h + 1) if h < H - 1 else (it + 1, 0)
                    prev = back(phase, it, h, 2)
                    if prev is not None:
                        transpose_probs(*prev, 0)
                        transpose_probs(*prev, 1)
                    if ahead:
                        score(*nxt, 0)
                    products = phase == DRAIN and h < 6 or phase == MID or phase == LAST or phase == FIRST and h >= 6
                    t, half = (it, 0) if h >= 6 else (it - 1, 0 if h < 2 else 1)
                    for i in range(2):
                        if products:
                            value_products(t, half, 2 * ((h - 6) % 4) + i)
                        if prev is not None:
                            transpose_probs(*prev, 2 + i)
                    if ahead:
                        score(*nxt, 1)
                    if h == 2 and to_route(it) is not None:
                        transpose_rows(to_route(it), 2 * NT if phase == DRAIN else 2 * it + 2)
                    if h == 3 and to_route(it) is not None:
                        find_logits(to_route(it))
                    if phase in (FIRST, MID) and h == 4:
                        transpose_queries(it + 1, 0)
                    if phase != FIRST and h == 6:
                        transpose_out(phase, it - 1)
                    if phase != DRAIN and h == 0:
                        transpose_queries(it, 1)

            tiles(pe, tile)
            transpose_rows(NT - 1, 2 * NT)
            find_logits(NT - 1)
            rank(NT - 1)


def expert_ffn(nc, x1, w1, b1, w2, b2, out, slots_x, slots_y, routing):
    pick12, pos, diff, ahead, scattered = routing
    N, D = x1.shape
    E, _, HID = w1.shape
    P = 128
    NT = N // P
    TOPK = 2
    RES = 4
    DC = D // P
    HC = HID // P
    BANK = 512
    TILES = slots_y.shape[0] // P
    REGION = N + P
    assert TILES >= N * TOPK // P + E - 1 and TILES % 2 == 0 and N // P <= E
    FEWEST = N * TOPK // P // 2
    FEWEST_EARLY = (E - 1) // 2
    W1C, W2C = DC * HID, HC * D
    WC = W1C + W2C

    x1_p = x1.rearrange("(t p) d -> p t d", p=P)
    out_t = out.rearrange("(t p) d -> t p d", p=P)
    w1_p = w1.rearrange("e (k p) h -> e p k h", p=P)
    w2_p = w2.rearrange("e (p c) d -> e p (c d)", c=HC)
    sy_t = slots_y.rearrange("(i p) d -> i p d", p=P)

    ctx = ExitStack()
    with ctx:
        def sb(name, shape, dt):
            return ctx.enter_context(nc.sbuf_tensor(name, shape, dt))

        def sem(name):
            return ctx.enter_context(nc.semaphore(name))

        w_raw = sb("w_raw", [P, 2, WC], F32)
        w_hi = sb("w_hi", [P, 2 * WC], F32R)
        w_lo = sb("w_lo", [P, 2 * WC], F32R)
        b1_bc = sb("b1_bc", [P, 2 * HID], F32)
        b2_bc = sb("b2_bc", [P, 2 * D], F32)
        x1_all = sb("x1_all", [P, NT, D], F32)
        ident2 = sb("ident2", [P, P], F32)
        idle = sb("idle", [P, P], BF16)
        table = sb("table", [P, 5, NT, E], F32)
        small = sb("small", [P, 8, NT], F32)
        place_fp = sb("place_fp", [P, TOPK, NT], F32)
        place_of = sb("place_of", [P, TOPK, NT], U32)
        tile_iota = sb("tile_iota", [1, TILES, E], F32)
        ended = sb("ended", [1, TILES, E], F32)
        tile_expert = sb("tile_expert", [1, TILES], F32)
        tile_expert_i = sb("tile_expert_i", [1, TILES], I32)
        tile_row = sb("tile_row", [1, TILES], F32)
        tiles_before = sb("tiles_before", [1, TILES], F32)
        tile_row_i = sb("tile_row_i", [1, TILES], I32)
        region_end_i = sb("region_end_i", [1, E], I32)
        tile_end_i = sb("tile_end_i", [1, E], I32)
        over_pairs = sb("over_pairs", [1, TILES // 2], F32)
        early_fp = sb("early_fp", [1, 2], F32)
        early_i = sb("early_i", [1, 2], I32)
        n_pairs = sb("n_pairs", [1, 1], F32)
        n_pairs_i = sb("n_pairs_i", [1, 1], I32)
        x_in_sb = sb("x_in_sb", [P, 2, D], F32)
        xT_hi = sb("xT_hi", [P, 2, DC * P], F32R)
        xT_lo = sb("xT_lo", [P, 2, DC * P], F32R)
        hid = sb("hid", [P, 2, HID], F32)
        hT_hi = sb("hT_hi", [P, 2, HID], F32R)
        hT_lo = sb("hT_lo", [P, 2, HID], F32R)
        y_sb = sb("y_sb", [P, 2, D], F32)
        at12 = hid[:, 0, 0:TOPK * NT * E].rearrange("p (k t e) -> p k t e", k=TOPK, e=E)
        zero_rows = y_sb[:, 0, :]
        got = [[w_raw[:, k, i * D:i * D + D] for i in range(NT)] for k in range(TOPK)]
        res = [hid[:, 0, i * D:i * D + D] for i in range(RES)]
        part = [hid[:, 1, i * D:i * D + D] for i in range(RES)]

        tmp, iota_j, tri = (table[:, i] for i in range(3))
        begin_e, tiles_e, end_e, base_e, count_e = (table[:, 3, i, :] for i in range(5))
        ediff, wt1, wt2, first, second, wt_a, wt_b, own_wt = (small[:, i, :] for i in range(8))

        h_ps = ctx.enter_context(nc.psum_tensor("h_ps", [P, HID], F32))
        ht_ps = ctx.enter_context(nc.psum_tensor("ht_ps", [P, HID], F32))
        y_ps = [ctx.enter_context(nc.psum_tensor(f"y_ps{i}", [P, BANK], F32)) for i in range(2)]
        xt_ps = ctx.enter_context(nc.psum_tensor("xt_ps", [P, BANK], F32))

        x1_in = sem("x1_in")
        const_step, const_ready = sem("const_step"), sem("const_ready")
        step, ediff_ready, table_ready = sem("step"), sem("ediff_ready"), sem("table_ready")
        zeros_ready = sem("zeros_ready")
        ends_ready, first_padded, padded = sem("ends_ready"), sem("first_padded"), sem("padded")
        places_ready = sem("places_ready")
        w1_in, w2_in, b1_in, b2_in = ([sem(f"{n}_in{i}") for i in range(2)] for n in ("w1", "w2", "b1", "b2"))
        pool_waited = sem("pool_waited")
        hi_ready = [sem("w1_hi_ready"), sem("w2_hi_ready")]
        b_seen = [sem("b1_seen"), sem("b2_seen")]
        w1_ready, w2_ready = sem("w1_ready"), sem("w2_ready")
        sx_in = [sem(f"sx_in{i}") for i in range(2)]
        xt_done, x_hi, x_lo = sem("xt_done"), sem("x_hi"), sem("x_lo")
        h_done, h_biased, gelu_done = sem("h_done"), sem("h_biased"), sem("gelu_done")
        ht_done, h_hi, h_lo = sem("ht_done"), sem("h_hi"), sem("h_lo")
        y_done, y_biased = sem("y_done"), sem("y_biased")
        sy_out = [sem(f"sy_out{i}") for i in range(2)]
        gathered = [sem(f"gathered{i}") for i in range(NT)]
        part_ready, res_ready = sem("part_ready"), sem("res_ready")
        stored = [sem(f"stored{i}") for i in range(RES)]

        def wait(eng, s, value):
            if not isinstance(value, int) or value > 0:
                eng.wait_ge(s, value)

        def pairs_of(eng):
            return eng.value_load(n_pairs_i[0:1, 0:1], min_val=0, max_val=TILES // 2 - FEWEST) + FEWEST

        def steps(eng, pair):
            pair(0, 0)
            pair(1, 1)
            pairs = pairs_of(eng)
            with eng.Fori(2, TILES // 2 - 1) as j:
                with eng.If(j < pairs - 1):
                    pair(1, j)
            pairs = pairs_of(eng)
            pair(2, pairs - 1)
            pair(3, pairs)

        def has(phase, i, d):
            if phase == 0:
                return i >= d
            if phase == 2:
                return i - d < 2
            if phase == 3:
                return i - d < 0
            return True

        def expert_of(eng, tile):
            return eng.value_load(tile_expert_i[0:1, bass.ds(tile, 1)], min_val=0, max_val=E - 1)

        SHARED = 10

        def fill_up(eng, e, done):
            end = eng.value_load(region_end_i[0:1, bass.ds(e, 1)], min_val=0, max_val=E * REGION - P)
            eng.dma_start(slots_x[bass.ds(end, P), :], zero_rows).then_inc(done, 16)

        block = ctx.enter_context(nc.Block())

        @block.sync
        def _(sp):
            def later(e):
                return not isinstance(e, int) or e >= 2

            def load_up(e, i):
                if later(e):
                    sp.wait_ge(w1_ready, e - 1)
                sp.dma_start(w_raw[:, i, 0:W1C].rearrange("p (k h) -> p k h", k=DC),
                             w1_p[bass.ds(e, 1)].rearrange("a p k h -> p (a k) h")).then_inc(w1_in[i], 16)

            def load_down(e, i):
                if later(e):
                    sp.wait_ge(w2_ready, e - 1)
                sp.dma_start(w_raw[:, i, W1C:WC], w2_p[bass.ds(e, 1)].rearrange("a p n -> p (a n)")).then_inc(w2_in[i], 16)

            def load_bias(e, i, src, dst, width, used, into):
                if later(e):
                    done = sp.value_load(tile_end_i[0:1, bass.ds(e - 2, 1)], min_val=1, max_val=TILES)
                    sp.wait_ge(used, done)
                sp.dma_start(dst[:, i * width:i * width + width], src[bass.ds(e, 1), :].to_broadcast([P, width])
                             ).then_inc(into[i], 16)

            def load_up_bias(e, i):
                load_bias(e, i, b1, b1_bc, HID, h_biased, b1_in)

            def load_down_bias(e, i):
                load_bias(e, i, b2, b2_bc, D, y_biased, b2_in)

            load_up(0, 0)
            sp.wait_ge(zeros_ready, 1)
            sp.wait_ge(ends_ready, 1)
            fill_up(sp, 0, first_padded)
            fill_up(sp, 2, first_padded)
            load_up_bias(0, 0)
            load_down(0, 0)
            load_down_bias(0, 0)
            load_up(1, 1)
            with sp.Fori(2, SHARED // 2) as j:
                fill_up(sp, 2 * j, padded)
            with sp.Fori(SHARED, E) as e:
                fill_up(sp, e, padded)
            load_up_bias(1, 1)
            load_down(1, 1)
            load_down_bias(1, 1)
            sp.wait_ge(table_ready, 1)
            for i in range(2):
                sp.wait_ge(sx_in[i], 16)

            load_up(2, 0)
            load_up(3, 1)
            load_down(2, 0)
            load_up_bias(2, 0)
            with sp.Fori(2, E // 2) as j:
                for i in range(2):
                    load_up(2 * j + i, i)
                    load_down(2 * j + i - 1, 1 - i)
                    load_up_bias(2 * j + i - 1, 1 - i)
                    load_down_bias(2 * j + i - 2, i)
            load_down(E - 1, 1)
            load_up_bias(E - 1, 1)
            load_down_bias(E - 2, 0)
            load_down_bias(E - 1, 1)
            sp.dma_start(x1_all[:, :, :], x1_p).then_inc(x1_in, 16)
            for t in range(NT):
                sp.wait_ge(res_ready, t + 1)
                sp.dma_start(out_t[t], res[t % RES]).then_inc(stored[t % RES], 16)
            for i in range(RES):
                sp.wait_ge(stored[i], 16 * NT // RES)

        @block.gpsimd
        def _(pool):
            n_c = [0]

            def const(ins):
                n_c[0] += 1
                ins.then_inc(const_step, 1)
                pool.wait_ge(const_step, n_c[0])

            const(nc.gpsimd.memset(ident2[:, :], 0.0))
            nc.gpsimd.affine_select(out=ident2[:, :], in_=ident2[:, :], compare_op=ALU.not_equal, fill=1.0, base=0,
                                    pattern=[[-1, P]], channel_multiplier=1)
            nc.gpsimd.memset(zero_rows, 0.0).then_inc(zeros_ready, 1)
            nc.gpsimd.memset(idle[:, :], 1.0)
            nc.gpsimd.iota(begin_e, pattern=[[REGION, E]], base=0, channel_multiplier=0, allow_small_or_imprecise_dtypes=True)
            nc.gpsimd.iota(iota_j, pattern=[[0, E], [P, NT]], base=0, channel_multiplier=0, allow_small_or_imprecise_dtypes=True)
            nc.gpsimd.iota(tile_iota[:, :, :], pattern=[[1, TILES], [0, E]], base=0, channel_multiplier=0,
                           allow_small_or_imprecise_dtypes=True)
            const(nc.gpsimd.memset(tri, 1.0))
            nc.gpsimd.affine_select(out=tri, in_=tri, compare_op=ALU.is_ge, fill=0.0, base=0,
                                    pattern=[[1, E], [-1, E]], channel_multiplier=0).then_inc(const_ready, 1)

            def split(e, i, j, second):
                at, to, w_in, used, ready = ((0, W1C, w1_in, h_done, w1_ready),
                                             (W1C, WC, w2_in, y_done, w2_ready))[second]
                if not isinstance(e, int) or e >= 2:
                    done = pool.value_load(tile_end_i[0:1, bass.ds(e - 2, 1)], min_val=1, max_val=TILES)
                    pool.wait_ge(used, done)
                pool.wait_ge(w_in[i], 16 * j + 16)
                pool.sem_inc(pool_waited, 1)
                high, low = w_hi[:, i * WC + at:i * WC + to], w_lo[:, i * WC + at:i * WC + to]
                nc.gpsimd.tensor_scalar(high, w_raw[:, i, at:to], 1.0, 0.0, ALU.mult, ALU.add).then_inc(hi_ready[second], 1)
                pool.wait_ge(hi_ready[second], e + 1)
                pool.sem_inc(pool_waited, 1)
                nc.gpsimd.tensor_tensor(out=low, in0=w_raw[:, i, at:to], in1=high.bitcast(F32),
                                        op=ALU.subtract).then_inc(ready, 1)
                see_bias(i, j, second)

            def see_bias(i, j, second):
                pool.wait_ge((b1_in, b2_in)[second][i], 16 * j + 16)
                pool.sem_inc(b_seen[second], 1)

            split(0, 0, 0, False)
            split(0, 0, 0, True)
            split(1, 1, 0, False)
            split(1, 1, 0, True)
            pool.wait_ge(table_ready, 1)
            split(2, 0, 1, False)
            split(3, 1, 1, False)
            split(2, 0, 1, True)
            with pool.Fori(2, E // 2) as j:
                split(2 * j, 0, j, False)
                split(2 * j - 1, 1, j - 1, True)
                split(2 * j + 1, 1, j, False)
                split(2 * j, 0, j, True)
            split(E - 1, 1, E // 2 - 1, True)

            def gather(k):
                for t in range(NT):
                    pool.indirect_dma_start(out=got[k][t], out_offset=None, in_=slots_y[:, :],
                                            in_offset=bass.IndirectOffsetOnAxis(ap=place_of[:, k, t:t + 1], axis=0)
                                            ).then_inc(gathered[t], 16)

            pool.wait_ge(places_ready, 1)
            early = [pool.value_load(early_i[0:1, i:i + 1], min_val=0, max_val=TILES // 2 - FEWEST_EARLY) + FEWEST_EARLY
                     for i in range(2)]
            for i in range(2):
                pool.wait_ge(sy_out[i], 16 * early[i])
            pool.sem_inc(pool_waited, 1)
            gather(0)
            pairs = pairs_of(pool)
            for i in range(2):
                pool.wait_ge(sy_out[i], 16 * pairs)
            pool.sem_inc(pool_waited, 1)
            gather(1)

        @block.scalar
        def _(act):
            act.wait_ge(zeros_ready, 1)
            act.wait_ge(ends_ready, 1)
            fill_up(act, 1, first_padded)
            fill_up(act, 3, first_padded)
            with act.Fori(2, SHARED // 2) as j:
                fill_up(act, 2 * j + 1, padded)
            nc.scalar.activation(ediff, diff[:, :], ACT.Exp).then_inc(ediff_ready, 1)
            def pair(phase, j):
                for i in range(2):
                    s = 2 * j + i
                    if has(phase, i, 0):
                        if has(phase, i, -2):
                            if isinstance(s, int) and s == 2:
                                act.wait_ge(padded, 16 * (E - 4))
                            act.wait_ge(xt_done, s + 1)
                            load_rows(s + 2, i)
                    if has(phase, i, -1):
                        x_high(s + 1, 1 - i)
                    if has(phase, i, 0):
                        act.wait_ge(h_biased, s + 1)
                        nc.scalar.activation(hid[:, i, :], hid[:, i, :], ACT.Gelu).then_inc(gelu_done, 1)
                    if has(phase, i, 1):
                        act.wait_ge(ht_done, s)
                        wait(act, y_done, s - 2)
                        nc.scalar.copy(hT_hi[:, 1 - i, :], ht_ps[:, :]).then_inc(h_hi, 1)
                    if has(phase, i, 2):
                        act.wait_ge(y_biased, s - 1)
                        act.dma_start(sy_t[s - 2], y_sb[:, i, :]).then_inc(sy_out[i], 16)

            def load_rows(t, i):
                row = act.value_load(tile_row_i[0:1, bass.ds(t, 1)], min_val=0, max_val=E * REGION - P)
                act.dma_start(x_in_sb[:, i, :], slots_x[bass.ds(row, P), :]).then_inc(sx_in[i], 16)

            def x_high(t, i):
                act.wait_ge(xt_done, t + 1)
                wait(act, h_done, t - 1)
                nc.scalar.copy(xT_hi[:, i, :], xt_ps[:, 0:DC * P]).then_inc(x_hi, 1)

            act.wait_ge(table_ready, 1)
            act.wait_ge(first_padded, 16 * 4)
            act.wait_ge(scattered, 16 * TOPK * NT)
            for i in range(2):
                load_rows(i, i)
            x_high(0, 0)
            steps(act, pair)

        @block.vector
        def _(dve):
            n = [0]

            def do(ins):
                n[0] += 1
                ins.then_inc(step, 1)
                dve.wait_ge(step, n[0])

            tt, ts, red = nc.vector.tensor_tensor, nc.vector.tensor_scalar, nc.vector.tensor_reduce

            def over_tiles(v, tiles):
                return v.unsqueeze(1).to_broadcast([P, tiles, E])

            nc.vector.tensor_copy(region_end_i[:, :], ahead[0:1, :]).then_inc(ends_ready, 1)

            dve.wait_ge(const_ready, 1)
            do(tt(count_e, ahead[:, :], begin_e, ALU.subtract))
            do(tt(tmp, count_e.unsqueeze(2).to_broadcast([P, E, NT]), iota_j, ALU.is_gt))
            do(red(out=tiles_e, in_=tmp, axis=AX.X, op=ALU.add))
            do(ts(tiles_e, tiles_e, 1.0, None, ALU.max))
            do(tt(tmp, tri, tiles_e.unsqueeze(1).to_broadcast([P, E, E]), ALU.mult))
            do(red(out=end_e, in_=tmp, axis=AX.X, op=ALU.add))
            do(tt(ended[:, :, :], end_e[0:1].unsqueeze(1).to_broadcast([1, TILES, E]), tile_iota[:, :, :], ALU.is_le))
            do(red(out=tile_expert[:, :], in_=ended[:, :, :], axis=AX.X, op=ALU.add))
            do(tt(ended[:, :, :], ended[:, :, :], tiles_e[0:1].unsqueeze(1).to_broadcast([1, TILES, E]), ALU.mult))
            do(red(out=tiles_before[:, :], in_=ended[:, :, :], axis=AX.X, op=ALU.add))
            do(tt(tiles_before[:, :], tile_iota[:, :, 0], tiles_before[:, :], ALU.subtract))
            do(ts(tiles_before[:, :], tiles_before[:, :], 0.0, float(NT - 1), ALU.max, ALU.min))
            do(ts(tile_expert[:, :], tile_expert[:, :], float(E - 1), None, ALU.min))
            do(ts(tile_row[:, :], tile_expert[:, :], float(REGION // P), None, ALU.mult))
            do(tt(tile_row[:, :], tile_row[:, :], tiles_before[:, :], ALU.add))
            do(ts(tile_row_i[:, :], tile_row[:, :], float(P), None, ALU.mult))
            do(nc.vector.tensor_copy(tile_end_i[:, :], end_e[0:1]))
            do(tt(over_pairs[:, :], tile_iota[:, 0:TILES:2, 0], end_e[0:1, E - 1:E].to_broadcast([1, TILES // 2]), ALU.is_lt))
            do(red(out=n_pairs[:, :], in_=over_pairs[:, :], axis=AX.X, op=ALU.add))
            do(ts(n_pairs_i[:, :], n_pairs[:, :], float(FEWEST), None, ALU.subtract))
            nc.vector.tensor_copy(tile_expert_i[:, :], tile_expert[:, :]).then_inc(table_ready, 1)

            do(tt(base_e, end_e, tiles_e, ALU.subtract))
            do(nc.vector.scalar_tensor_tensor(out=base_e, in0=base_e, scalar=float(P), in1=begin_e, op0=ALU.mult, op1=ALU.subtract))
            do(tt(pos[:, :, :], pos[:, :, :], over_tiles(base_e, NT), ALU.add))
            do(tt(at12, pick12[:, :, :, :], pos[:, :, :].unsqueeze(1).to_broadcast([P, TOPK, NT, E]), ALU.mult))
            do(red(out=place_fp[:, :, :], in_=at12, axis=AX.X, op=ALU.add))
            for k, op in enumerate((ALU.min, ALU.max)):
                do(tt(place_of[:, k, :], place_fp[:, 0, :], place_fp[:, 1, :], op))
            for i in range(2):
                do(tt(over_pairs[:, :], tile_iota[:, i:TILES:2, 0], end_e[0:1, E - 2:E - 1].to_broadcast([1, TILES // 2]), ALU.is_lt))
                do(red(out=early_fp[:, i:i + 1], in_=over_pairs[:, :], axis=AX.X, op=ALU.add))
            ts(early_i[:, :], early_fp[:, :], float(FEWEST_EARLY), None, ALU.subtract).then_inc(places_ready, 1)

            def x_low(t, i):
                dve.wait_ge(x_hi, t + 1)
                wait(dve, h_done, t - 1)
                tt(xT_lo[:, i, :], xt_ps[:, 0:DC * P], xT_hi[:, i, :].bitcast(F32), ALU.subtract).then_inc(x_lo, 1)

            def pair(phase, j):
                for i in range(2):
                    s = 2 * j + i
                    if has(phase, i, 0):
                        e = expert_of(dve, s)
                        dve.wait_ge(b_seen[0], e + 1)
                        dve.wait_ge(h_done, s + 1)
                        wait(dve, ht_done, s - 1)
                        tt(hid[:, i, :], h_ps[:, :], b1_bc[:, bass.ds((e % 2) * HID, HID)], ALU.add).then_inc(h_biased, 1)
                    if has(phase, i, -1):
                        x_low(s + 1, 1 - i)
                    if has(phase, i, 1):
                        dve.wait_ge(h_hi, s)
                        wait(dve, y_done, s - 2)
                        tt(hT_lo[:, 1 - i, :], ht_ps[:, :], hT_hi[:, 1 - i, :].bitcast(F32), ALU.subtract).then_inc(h_lo, 1)
                    if has(phase, i, 2):
                        e = expert_of(dve, s - 2)
                        dve.wait_ge(b_seen[1], e + 1)
                        dve.wait_ge(y_done, s - 1)
                        wait(dve, sy_out[i], 16 * (j - 1))
                        tt(y_sb[:, i, :], y_ps[i][:, 0:D], b2_bc[:, bass.ds((e % 2) * D, D)], ALU.add).then_inc(y_biased, 1)

            x_low(0, 0)
            steps(dve, pair)
            dve.wait_ge(ediff_ready, 1)
            do(ts(wt1, ediff, 1.0, None, ALU.add))
            do(nc.vector.reciprocal(wt1, wt1))
            do(tt(wt2, ediff, wt1, ALU.mult))
            do(tt(first, place_fp[:, 0, :], place_fp[:, 1, :], ALU.is_lt))
            do(ts(second, first, -1.0, 1.0, ALU.mult, ALU.add))
            for to, own, other in ((wt_a, first, second), (wt_b, second, first)):
                do(tt(to, wt1, own, ALU.mult))
                do(tt(own_wt, wt2, other, ALU.mult))
                do(tt(to, to, own_wt, ALU.add))
            dve.wait_ge(x1_in, 16)
            for t in range(NT):
                dve.wait_ge(gathered[t], 16 * TOPK)
                nc.vector.scalar_tensor_tensor(out=part[t % RES], in0=got[0][t], scalar=wt_a[:, t:t + 1], in1=x1_all[:, t, :],
                                               op0=ALU.mult, op1=ALU.add).then_inc(part_ready, 1)
                dve.wait_ge(part_ready, t + 1)
                if t >= RES:
                    dve.wait_ge(stored[t % RES], 16 * (t // RES))
                nc.vector.scalar_tensor_tensor(out=res[t % RES], in0=got[1][t], scalar=wt_b[:, t:t + 1], in1=part[t % RES],
                                               op0=ALU.mult, op1=ALU.add).then_inc(res_ready, 1)

        @block.tensor
        def _(pe):
            pe.wait_ge(const_ready, 1)

            def keep_warm(rounds):
                with pe.Fori(0, rounds):
                    for i in range(8):
                        nc.tensor.matmul(y_ps[0][:, 0:P], idle[:, :], idle[:, :], start=True, stop=True)

            pe.wait_ge(table_ready, 1)
            keep_warm(3)

            def transpose_rows(t, i, j):
                pe.wait_ge(sx_in[i], 16 * j + 16)
                wait(pe, x_lo, t)
                for k in range(DC):
                    last = nc.tensor.transpose(xt_ps[:, k * P:k * P + P], x_in_sb[:, i, k * P:k * P + P], ident2[:, :])
                last.then_inc(xt_done, 1)

            def up(t, i):
                e = expert_of(pe, t)
                base = (e % 2) * WC
                pe.wait_ge(w1_ready, e + 1)
                wait(pe, h_biased, t)
                pe.wait_ge(x_lo, t + 1)
                for half in range(HID // BANK):
                    terms = [(x, w, k) for k in range(DC) for x, w in ((xT_hi, w_hi), (xT_hi, w_lo), (xT_lo, w_hi))]
                    for n_, (x, w, k) in enumerate(terms):
                        last = nc.tensor.matmul(h_ps[:, half * BANK:half * BANK + BANK], x[:, i, k * P:k * P + P],
                                                w[:, bass.ds(base + k * HID + half * BANK, BANK)],
                                                start=n_ == 0, stop=n_ == len(terms) - 1)
                last.then_inc(h_done, 1)

            def transpose_hidden(t, i):
                pe.wait_ge(gelu_done, t + 1)
                wait(pe, h_lo, t)
                for c in range(HC):
                    last = nc.tensor.transpose(ht_ps[:, c * P:c * P + P], hid[:, i, c:HID:HC], ident2[:, :])
                last.then_inc(ht_done, 1)

            def down(t, i):
                e = expert_of(pe, t)
                base = (e % 2) * WC + W1C
                pe.wait_ge(w2_ready, e + 1)
                pe.wait_ge(h_lo, t + 1)
                wait(pe, y_biased, t - 1)
                for c in range(HC):
                    for n_, (x, w) in enumerate(((hT_hi, w_hi), (hT_hi, w_lo), (hT_lo, w_hi))):
                        last = nc.tensor.matmul(y_ps[i][:, 0:D], x[:, i, c * P:c * P + P], w[:, bass.ds(base + c * D, D)],
                                                start=c == 0 and n_ == 0, stop=c == HC - 1 and n_ == 2)
                last.then_inc(y_done, 1)

            def pair(phase, j):
                for i in range(2):
                    s = 2 * j + i
                    if has(phase, i, 0):
                        up(s, i)
                    if has(phase, i, -1):
                        transpose_rows(s + 1, 1 - i, j + i)
                    if has(phase, i, 1):
                        transpose_hidden(s - 1, 1 - i)
                    if has(phase, i, 2):
                        down(s - 2, i)

            transpose_rows(0, 0, 0)
            steps(pe, pair)


def layer(nc, x, adj, x2, v, wg, bg, w1, b1, w2, b2, out):
    P = 128
    N, D = x.shape
    E = w1.shape[0]
    tiles = -(-(N * 2 // P + E - 1) // (N // P)) * (N // P)
    x1 = nc.dram_tensor("x1", [N, D], F32).ap()
    slots_x = nc.dram_tensor("slots_x", [E * (N + P), D], F32).ap()
    slots_y = nc.dram_tensor("slots_y", [tiles * P, D], F32).ap()
    with nc.sbuf_tensor("pick12", [P, 2, N // P, E], F32) as pick12, nc.sbuf_tensor("pos_all", [P, N // P, E], F32) as pos_all, \
            nc.sbuf_tensor("diff_all", [P, N // P], F32) as diff_all, nc.sbuf_tensor("ahead", [P, E], F32) as ahead, \
            nc.semaphore("scattered") as scattered:
        routing = (pick12, pos_all, diff_all, ahead, scattered)
        attend_and_route(nc, x, adj, x2, v, wg, bg, x1, slots_x, slots_y, routing)
        expert_ffn(nc, x1, w1, b1, w2, b2, out, slots_x, slots_y, routing)


_INS = ["x", "adj", "L0_gnn_x2", "L0_gnn_v", "L0_ffn_Wg", "L0_ffn_bg", "L0_ffn_W1", "L0_ffn_b1", "L0_ffn_W2", "L0_ffn_b2"]


def kernel(**inputs):
    import numpy as _np
    import concourse.bacc as _bacc
    from concourse import mybir as _mybir
    from concourse.bass_utils import run_bass_kernel_spmd as _run

    nc = _bacc.Bacc("TRN2", target_bir_lowering=False, num_devices=1)
    arrays, args = {}, []
    for name in _INS:
        a = _np.ascontiguousarray(inputs[name])
        arrays[f"in_{name}"] = a
        args.append(nc.dram_tensor(f"in_{name}", a.shape, _mybir.dt.from_np(a.dtype), kind="ExternalInput").ap())
    out = nc.dram_tensor("out", inputs["x"].shape, _mybir.dt.float32, kind="ExternalOutput").ap()
    layer(nc, *args, out)
    return _run(nc, [arrays], core_ids=[0]).results[0]["out"]
```
